# Optimizing a Trainium2 kernel written in Bass

```python
import numpy as np
import jax
import jax.numpy as jnp

def _softmax(x, axis=-1):
    return jax.nn.softmax(x, axis=axis)

def _gelu(x):
    return jax.nn.gelu(x, approximate=True)

def _silu(x):
    return jax.nn.silu(x)

def _sigmoid(x):
    return jax.nn.sigmoid(x)

def _layernorm(x, axis=-1, eps=1e-05):
    m = jnp.mean(x, axis=axis, keepdims=True)
    v = jnp.var(x, axis=axis, keepdims=True)
    return (x - m) / jnp.sqrt(v + eps)

def _scatter_add(tgt, idx, src, axis=0):
    return tgt.at[idx].add(src)

def _segment_sum(src, seg, n):
    return jax.ops.segment_sum(src, seg, n)
kernel_name = 'mk_gnn_resnorm_d4_gnn_r8_aa5807'

def setup_inputs(seed: int=0):
    np.random.seed(seed)
    _w = jnp.asarray

    def _rec_inputs():
        import jax
        import jax.numpy as jnp
        _gk = jax.random.key(seed)
        x = -0.0005121 + 1.001 * jax.random.normal(jax.random.fold_in(_gk, 1), (12500, 32), jnp.float32)
        src = jax.random.randint(jax.random.fold_in(_gk, 2), (400000,), 0, 12500, jnp.int32)
        dst = jnp.minimum((12500 * jax.random.uniform(jax.random.fold_in(_gk, 3), (400000,)) ** 2.0).astype(jnp.int32), 99999)
        _o = jnp.argsort(dst, stable=True)
        src = src[_o]
        dst = dst[_o]
        edge_attr_16 = 0.000254156 + 0.999948 * jax.random.normal(jax.random.fold_in(_gk, 12), (400000, 16), jnp.float32)
        edge_attr_2 = jax.random.uniform(jax.random.fold_in(_gk, 13), (400000, 2), jnp.float32, 0.0, 1)
        return (x, src, dst, edge_attr_16, edge_attr_2)
    x, src, dst, edge_attr_16, edge_attr_2 = _rec_inputs()

    def _L0_gnn_setup():
        import jax, jax.numpy as jnp
        import numpy as np
        N_NODES = 12500
        N_EDGES = 200000
        DIM1 = 32
        LEAKY_SLOPE = 0.01
        key = jax.random.key(seed)
        k1, k2, k3, k4 = jax.random.split(key, 4)
        h = jax.random.normal(k1, (N_NODES, DIM1), dtype=jnp.float32)
        attn_w = jax.random.normal(k2, (2 * DIM1,), dtype=jnp.float32) * (1.0 / np.sqrt(2 * DIM1))
        src = jax.random.randint(k3, (N_EDGES,), 0, N_NODES, dtype=jnp.int32)
        dst = jax.random.randint(k4, (N_EDGES,), 0, N_NODES, dtype=jnp.int32)
        return {'h': h, 'attn_w': attn_w, 'src': src, 'dst': dst}
    _L0_gnn_all = _L0_gnn_setup()
    _L0_gnn_in = {k: v for k, v in _L0_gnn_all.items() if k in ('attn_w',)}
    del _L0_gnn_all

    def _L1_gnn_setup():
        import jax, jax.numpy as jnp
        import numpy as np
        N_NODES = 6250
        N_EDGES = 100000
        NODE_D, EDGE_D = (32, 16)
        FLOW_IN, FLOW_H, FLOW_OUT = (2 * NODE_D + EDGE_D, 64, 64)
        NODE_H, NODE_OUT = (64, 32)

        def _mlp(h, W1, b1, W2, b2):
            h = jax.nn.relu(h @ W1 + b1)
            return h @ W2 + b2
        key = jax.random.key(seed)
        ks = jax.random.split(key, 8)
        return {'x': jax.random.normal(ks[0], (N_NODES, NODE_D), dtype=jnp.float32), 'edge_index': jax.random.randint(ks[1], (2, N_EDGES), 0, N_NODES, dtype=jnp.int64), 'edge_attr': jax.random.normal(ks[2], (N_EDGES, EDGE_D), dtype=jnp.float32), 'Wf1': jax.random.normal(ks[3], (FLOW_IN, FLOW_H), dtype=jnp.float32) * (1.0 / np.sqrt(FLOW_IN)), 'bf1': jnp.zeros((FLOW_H,), dtype=jnp.float32), 'Wf2': jax.random.normal(ks[4], (FLOW_H, FLOW_OUT), dtype=jnp.float32) * (1.0 / np.sqrt(FLOW_H)), 'bf2': jnp.zeros((FLOW_OUT,), dtype=jnp.float32), 'Wn1': jax.random.normal(ks[5], (FLOW_OUT, NODE_H), dtype=jnp.float32) * (1.0 / np.sqrt(FLOW_OUT)), 'bn1': jnp.zeros((NODE_H,), dtype=jnp.float32), 'Wn2': jax.random.normal(ks[6], (NODE_H, NODE_OUT), dtype=jnp.float32) * (1.0 / np.sqrt(NODE_H)), 'bn2': jnp.zeros((NODE_OUT,), dtype=jnp.float32)}
    _L1_gnn_all = _L1_gnn_setup()
    _L1_gnn_in = {k: v for k, v in _L1_gnn_all.items() if k in ('Wf1', 'bf1', 'Wf2', 'bf2', 'Wn1', 'bn1', 'Wn2', 'bn2')}
    del _L1_gnn_all

    def _L2_gnn_setup():
        import jax, jax.numpy as jnp
        import numpy as np
        import itertools
        N = 12500
        E = 200000
        DIM = 2
        K = 5
        K_TOT = K ** DIM
        IS_OPEN = True
        M_IN = 32
        M_OUT = 32
        S = 2 ** DIM

        def spline_basis_deg1(pseudo):
            scale = K - 1 if IS_OPEN else K
            p = pseudo * scale
            lo_f = jnp.floor(p)
            frac = p - lo_f
            lo = lo_f.astype(jnp.int32)
            strides = [K ** d for d in range(DIM)]
            bases, idxs = ([], [])
            for s in itertools.product((0, 1), repeat=DIM):
                b = jnp.ones(p.shape[0], p.dtype)
                flat = jnp.zeros(p.shape[0], jnp.int32)
                for d, sd in enumerate(s):
                    b = b * (frac[:, d] if sd else 1.0 - frac[:, d])
                    i = lo[:, d] + sd
                    i = jnp.clip(i, 0, K - 1) if IS_OPEN else jnp.mod(i, K)
                    flat = flat + i * strides[d]
                bases.append(b)
                idxs.append(flat)
            return (jnp.stack(bases, axis=1), jnp.stack(idxs, axis=1))
        key = jax.random.key(seed)
        k1, k2, k3, k4, k5, k6 = jax.random.split(key, 6)
        x = jax.random.normal(k1, (N, M_IN), dtype=jnp.float32)
        edge_index = jax.random.randint(k2, (2, E), 0, N, dtype=jnp.int64)
        pseudo = jax.random.uniform(k3, (E, DIM), dtype=jnp.float32)
        bound = 1.0 / np.sqrt(M_IN * K_TOT)
        weight = jax.random.uniform(k4, (K_TOT, M_IN, M_OUT), jnp.float32, -bound, bound)
        root_weight = jax.random.uniform(k5, (M_IN, M_OUT), jnp.float32, -bound, bound)
        bias = jax.random.uniform(k6, (M_OUT,), jnp.float32, -bound, bound)
        return {'x': x, 'edge_index': edge_index, 'pseudo': pseudo, 'weight': weight, 'root_weight': root_weight, 'bias': bias}
    _L2_gnn_all = _L2_gnn_setup()
    _L2_gnn_in = {k: v for k, v in _L2_gnn_all.items() if k in ('weight', 'root_weight', 'bias')}
    del _L2_gnn_all

    def _L3_gnn_setup():
        import jax, jax.numpy as jnp
        import numpy as np
        N = 12500
        E = 200000
        F_IN = 32
        F_OUT = 32
        key = jax.random.key(seed)
        k1, k2, k3, k4, k5 = jax.random.split(key, 5)
        x = jax.random.normal(k1, (N, F_IN), dtype=jnp.float32)
        edge_src = jax.random.randint(k2, (E,), 0, N, dtype=jnp.int32)
        edge_dst = jax.random.randint(k3, (E,), 0, N, dtype=jnp.int32)
        bound = 1.0 / np.sqrt(2 * F_IN)
        W = jax.random.uniform(k4, (2 * F_IN, F_OUT), minval=-bound, maxval=bound, dtype=jnp.float32)
        b = jax.random.uniform(k5, (F_OUT,), minval=-bound, maxval=bound, dtype=jnp.float32)
        return {'x': x, 'W': W, 'b': b, 'edge_src': edge_src, 'edge_dst': edge_dst}
    _L3_gnn_all = _L3_gnn_setup()
    _L3_gnn_in = {k: v for k, v in _L3_gnn_all.items() if k in ('W', 'b')}
    del _L3_gnn_all
    return {'x': x, 'src': src, 'dst': dst, 'edge_attr_16': edge_attr_16, 'edge_attr_2': edge_attr_2, 'L0_gnn_attn_w': _L0_gnn_in['attn_w'], 'L1_gnn_Wf1': _L1_gnn_in['Wf1'], 'L1_gnn_bf1': _L1_gnn_in['bf1'], 'L1_gnn_Wf2': _L1_gnn_in['Wf2'], 'L1_gnn_bf2': _L1_gnn_in['bf2'], 'L1_gnn_Wn1': _L1_gnn_in['Wn1'], 'L1_gnn_bn1': _L1_gnn_in['bn1'], 'L1_gnn_Wn2': _L1_gnn_in['Wn2'], 'L1_gnn_bn2': _L1_gnn_in['bn2'], 'L2_gnn_weight': _L2_gnn_in['weight'], 'L2_gnn_root_weight': _L2_gnn_in['root_weight'], 'L2_gnn_bias': _L2_gnn_in['bias'], 'L3_gnn_W': _L3_gnn_in['W'], 'L3_gnn_b': _L3_gnn_in['b']}

def reference(x, src, dst, edge_attr_16, edge_attr_2, L0_gnn_attn_w, L1_gnn_Wf1, L1_gnn_bf1, L1_gnn_Wf2, L1_gnn_bf2, L1_gnn_Wn1, L1_gnn_bn1, L1_gnn_Wn2, L1_gnn_bn2, L2_gnn_weight, L2_gnn_root_weight, L2_gnn_bias, L3_gnn_W, L3_gnn_b):
    import jax
    import jax.numpy as jnp

    def _L0_gnn_ref(h, attn_w, src, dst):
        import jax, jax.numpy as jnp
        import numpy as np
        N_NODES = 12500
        N_EDGES = 200000
        DIM1 = 32
        LEAKY_SLOPE = 0.01
        N, d = h.shape
        s_src = h @ attn_w[:d]
        s_dst = h @ attn_w[d:]
        e = s_src[src] + s_dst[dst]
        e = jnp.where(e >= 0, e, LEAKY_SLOPE * e)
        m = jax.ops.segment_max(e, dst, num_segments=N)
        ex = jnp.exp(e - m[dst])
        denom = jax.ops.segment_sum(ex, dst, num_segments=N)
        alpha = ex / denom[dst]
        out = jax.ops.segment_sum(h[src] * alpha[:, None], dst, num_segments=N)
        return out

    def _L1_gnn_ref(x, edge_index, edge_attr, Wf1, bf1, Wf2, bf2, Wn1, bn1, Wn2, bn2):
        import jax, jax.numpy as jnp
        import numpy as np
        N_NODES = 6250
        N_EDGES = 100000
        NODE_D, EDGE_D = (32, 16)
        FLOW_IN, FLOW_H, FLOW_OUT = (2 * NODE_D + EDGE_D, 64, 64)
        NODE_H, NODE_OUT = (64, 32)

        def _mlp(h, W1, b1, W2, b2):
            h = jax.nn.relu(h @ W1 + b1)
            return h @ W2 + b2
        past, future = (edge_index[0], edge_index[1])
        x_p = x[past]
        x_f = x[future]
        flow_fwd = jnp.concatenate([x_f, x_p, edge_attr], axis=1)
        flow_bwd = jnp.concatenate([x_p, x_f, edge_attr], axis=1)
        flow_total_in = jnp.concatenate([flow_fwd, flow_bwd], axis=0)
        flow_processed = _mlp(flow_total_in, Wf1, bf1, Wf2, bf2)
        dest = jnp.concatenate([future, past], axis=0)
        flow_total = jax.ops.segment_sum(flow_processed, dest, num_segments=x.shape[0])
        return _mlp(flow_total, Wn1, bn1, Wn2, bn2)

    def _L2_gnn_ref(x, edge_index, pseudo, weight, root_weight, bias):
        import jax, jax.numpy as jnp
        import numpy as np
        import itertools
        N = 12500
        E = 200000
        DIM = 2
        K = 5
        K_TOT = K ** DIM
        IS_OPEN = True
        M_IN = 32
        M_OUT = 32
        S = 2 ** DIM

        def spline_basis_deg1(pseudo):
            scale = K - 1 if IS_OPEN else K
            p = pseudo * scale
            lo_f = jnp.floor(p)
            frac = p - lo_f
            lo = lo_f.astype(jnp.int32)
            strides = [K ** d for d in range(DIM)]
            bases, idxs = ([], [])
            for s in itertools.product((0, 1), repeat=DIM):
                b = jnp.ones(p.shape[0], p.dtype)
                flat = jnp.zeros(p.shape[0], jnp.int32)
                for d, sd in enumerate(s):
                    b = b * (frac[:, d] if sd else 1.0 - frac[:, d])
                    i = lo[:, d] + sd
                    i = jnp.clip(i, 0, K - 1) if IS_OPEN else jnp.mod(i, K)
                    flat = flat + i * strides[d]
                bases.append(b)
                idxs.append(flat)
            return (jnp.stack(bases, axis=1), jnp.stack(idxs, axis=1))
        n = x.shape[0]
        row, col = (edge_index[0], edge_index[1])
        basis, idx = spline_basis_deg1(pseudo)
        x_j = x[col]
        h = jnp.zeros((n * K_TOT, x.shape[1]), dtype=x.dtype)
        for s in range(S):
            keys = row * K_TOT + idx[:, s]
            h = h + jax.ops.segment_sum(basis[:, s, None] * x_j, keys, num_segments=n * K_TOT)
        h = h.reshape(n, K_TOT, x.shape[1])
        out = jnp.einsum('nki,kio->no', h, weight)
        deg = jax.ops.segment_sum(jnp.ones(row.shape[0], x.dtype), row, num_segments=n)
        out = out / jnp.clip(deg, 1.0)[:, None]
        out = out + x @ root_weight + bias
        return out

    def _L3_gnn_ref(x, W, b, edge_src, edge_dst):
        import jax, jax.numpy as jnp
        import numpy as np
        N = 12500
        E = 200000
        F_IN = 32
        F_OUT = 32
        n = x.shape[0]
        msgs = x[edge_src]
        summed = jax.ops.segment_sum(msgs, edge_dst, num_segments=n)
        cnt = jax.ops.segment_sum(jnp.ones_like(edge_dst, dtype=x.dtype), edge_dst, num_segments=n)
        neigh_mean = summed / jnp.maximum(cnt, 1.0)[:, None]
        h = jnp.concatenate([x, neigh_mean], axis=1)
        return jax.nn.relu(h @ W + b)
    edge_index = jnp.stack([src, dst])
    x = _layernorm(x + _L0_gnn_ref(x, L0_gnn_attn_w, src, dst), axis=-1)
    x = _layernorm(x + _L1_gnn_ref(x, edge_index, edge_attr_16, L1_gnn_Wf1, L1_gnn_bf1, L1_gnn_Wf2, L1_gnn_bf2, L1_gnn_Wn1, L1_gnn_bn1, L1_gnn_Wn2, L1_gnn_bn2), axis=-1)
    x = _layernorm(x + _L2_gnn_ref(x, edge_index, edge_attr_2, L2_gnn_weight, L2_gnn_root_weight, L2_gnn_bias), axis=-1)
    x = _layernorm(x + _L3_gnn_ref(x, L3_gnn_W, L3_gnn_b, src, dst), axis=-1)
    return x

_drawn_inputs = setup_inputs


def setup_inputs(seed=0):
    import zlib

    import numpy as np

    out = dict(_drawn_inputs(seed))
    spreads = {'L1_gnn_bf1': (0.0, 0.1),
     'L1_gnn_bf2': (0.0, 0.1),
     'L1_gnn_bn1': (0.0, 2.0),
     'L1_gnn_bn2': (0.0, 0.8)}
    factors = {'edge_attr_2': 5.095, 'L2_gnn_weight': 2.685, 'L2_gnn_bias': 2.895}
    for name, (base, spread) in spreads.items():
        noise = np.random.default_rng([zlib.crc32(name.encode()), seed]).standard_normal(out[name].shape)
        drawn = base * np.exp(spread * noise) if base else spread * noise
        out[name] = jnp.asarray(drawn.astype(out[name].dtype))
    for name, factor in factors.items():
        out[name] = (out[name] * factor).astype(out[name].dtype)
    return out
```

```python
from contextlib import ExitStack

import numpy as np
import concourse.bass as bass
from concourse import mybir

F32 = mybir.dt.float32
I32 = mybir.dt.int32
I16 = mybir.dt.int16
ALU = mybir.AluOpType
ACT = mybir.ActivationFunctionType
AX = mybir.AxisListType.X

P = 128
N = 12500
E = 400000
D = 32
NB = -(-N // P)
NP = NB * P
TPC = 4
CE = P * TPC
RING = 4
CH = -(-E // (CE * RING)) * RING
EP = CH * CE
IT = CH // RING
EA = 16
FH = 64
HW = FH + 1
KS = 5
DUMP = NP
TR = NP + P
BIG = 1.0e30
SLOPE = 0.01
EPS = 1e-5
LAG = 2
GB = 7
NS = NB // GB
RG = 112
NG = CH // RG


def build(nc, t):
    with ExitStack() as top:
        of_layer = []

        def sbuf(ctx, name, shape, dt=F32):
            return ctx.enter_context(nc.sbuf_tensor(name, shape, dt))

        def psum(ctx, name, cols):
            return ctx.enter_context(nc.psum_tensor(name, [P, cols], F32))

        def sem(ctx, name):
            handle = nc.alloc_semaphore(name=name)
            if ctx is not top:
                of_layer.append(handle)
            return handle

        def clear_semaphores():
            nc.clear_and_free_semaphores(of_layer)
            nc.all_engine_barrier()
            of_layer.clear()

        def sems(ctx, name, n=RING):
            return [sem(ctx, f"{name}{r}") for r in range(n)]

        pe_went_on, dve_went_on, sp_went_on = (sem(top, n) for n in ("pe_went_on", "dve_went_on", "sp_went_on"))

        def went_on(eng, signal):
            eng.sem_inc(signal, 1)

        ranges_dram = nc.dram_tensor("ranges_dram", (CH, 4), I32, kind="Internal").ap()
        x_gathered = nc.dram_tensor("x_gathered", (CH, P, TPC * D), F32, kind="Internal").ap()
        flow_rows = nc.dram_tensor("flow_rows", (NP, 2 * FH), F32, kind="Internal").ap()
        flow_sums = [nc.dram_tensor(f"flow_sums{j}", (TR, HW), F32, kind="Internal").ap() for j in range(TPC)]
        spline_sums = [nc.dram_tensor(f"spline_sums{j}", (TR, D), F32, kind="Internal").ap() for j in range(TPC)]
        x3_rows = nc.dram_tensor("x3_rows", (NP, D), F32, kind="Internal").ap()

        src_chunks = t["src"].rearrange("(c p j) -> c p j", p=P, j=TPC)
        src_rows = t["src"].rearrange("(c o e) -> c o e", o=1, e=CE)
        dst_rows = t["dst"].rearrange("(c o e) -> c o e", o=1, e=CE)
        attr_chunks = t["edge_attr_16"].rearrange("(c p j) f -> c p (j f)", p=P, j=TPC)
        pseudo_chunks = t["edge_attr_2"].rearrange("(c p j) f -> c p (j f)", p=P, j=TPC)

        X = sbuf(top, "X", [P, NB, D])
        acc = sbuf(top, "acc", [P, NB, HW])
        dst_col = sbuf(top, "dst_col", [P, CH * TPC])
        uniq = sbuf(top, "uniq", [P, CH * TPC], I32)
        node_id = sbuf(top, "node_id", [P, NB])
        iota = sbuf(top, "iota", [P, NP], I16)
        ident = sbuf(top, "ident", [P, P])
        below = sbuf(top, "below", [P, P])
        dump_id = sbuf(top, "dump_id", [P, 1])
        ranges = sbuf(top, "ranges", [1, CH * 4], I32)
        deg_src = sbuf(top, "deg_src", [P, NB])
        deg_dst = sbuf(top, "deg_dst", [P, NB])

        def block_range(eng, regs, c):
            eng.load(regs, ranges[0:1, 4 * c:4 * c + 2] if isinstance(c, int) else ranges[0:1, bass.ds(4 * c, 2)])
            return (eng.snap(regs[0], min_val=0, max_val=NB - 1), eng.snap(regs[1], min_val=0, max_val=NB - 1))

        def cols(tensor, c, n):
            return tensor[:, bass.ds(c * n, n)]

        def one_hot_T(out, dst_row, b):
            return nc.vector.tensor_scalar(out.rearrange("n (j p) -> n j p", j=TPC),
                                           dst_row.rearrange("n (p j) -> n j p", j=TPC),
                                           node_id[:, bass.ds(b, 1)], None, ALU.is_equal)

        def one_hot(out, c, b):
            return nc.vector.tensor_tensor(
                out, iota[:, bass.ds(b * P, P)].unsqueeze(1).to_broadcast([P, TPC, P]),
                cols(dst_col, c, TPC).unsqueeze(2).to_broadcast([P, TPC, P]), ALU.is_equal)

        def add_to_block(b, width, sums):
            a = acc[:, bass.ds(b, 1), 0:width].rearrange("p o f -> p (o f)")
            return nc.vector.tensor_tensor(a, a, sums, ALU.add)

        def same_src(out, src_row, src_col):
            return nc.vector.tensor_tensor(out, src_row.rearrange("q (p j) -> q j p", j=TPC),
                                           src_col.unsqueeze(2).to_broadcast([P, TPC, P]), ALU.is_equal)

        with ExitStack() as ctx:
            dst_int = sbuf(ctx, "dst_int", [P, CH, TPC], I32)
            low = sbuf(ctx, "low", [P, CH])
            high = sbuf(ctx, "high", [P, CH])
            lh = sbuf(ctx, "lh", [P, NG, 4])
            lh_int = sbuf(ctx, "lh_int", [P, NG, 4], I32)
            ps = [psum(ctx, f"ps_range{k}", 512) for k in range(2)]
            loaded, x_loaded = sem(ctx, "dst_loaded"), sem(ctx, "x_loaded")
            consts, filled = sem(ctx, "consts"), sem(ctx, "filled")
            minmax, turned, reduced = sem(ctx, "minmax"), sem(ctx, "turned"), sem(ctx, "reduced")
            as_int, stored, back = sem(ctx, "as_int"), sem(ctx, "stored"), sem(ctx, "back")
            with nc.Block() as block:
                @block.sync
                def _(sp):
                    dst_cols = t["dst"].rearrange("(c p j) -> p c j", p=P, j=TPC)
                    for g in range(NG):
                        sp.dma_start(dst_int[:, g * RG:(g + 1) * RG, :],
                                     dst_cols[:, g * RG:(g + 1) * RG, :]).then_inc(loaded, 16)
                    sp.dma_start(X[:], t["x"].rearrange("(b p) f -> p b f", p=P)).then_inc(x_loaded, 16)
                    sp.wait_ge(as_int, 2)
                    sp.dma_start(ranges_dram.rearrange("(g q) k -> q g k", g=NG),
                                 lh_int[0:RG, :, :]).then_inc(stored, 16)
                    sp.wait_ge(stored, 16)
                    sp.dma_start(ranges[0:1, :], ranges_dram.rearrange("(o c) k -> o (c k)", o=1)).then_inc(back, 16)
                    sp.wait_ge(back, 16)
                    sp.wait_ge(x_loaded, 16)

                @block.gpsimd
                def _(pool):
                    pool.memset(ident[:], 0.0).then_inc(filled, 1)
                    pool.memset(below[:], 1.0).then_inc(filled, 1)
                    pool.iota(iota[:], [[1, NP]], base=0, channel_multiplier=0,
                              allow_small_or_imprecise_dtypes=True).then_inc(consts, 1)
                    pool.iota(node_id[:], [[P, NB]], base=0, channel_multiplier=1,
                              allow_small_or_imprecise_dtypes=True).then_inc(consts, 1)
                    pool.iota(dump_id[:], [[0, 1]], base=DUMP, channel_multiplier=1,
                              allow_small_or_imprecise_dtypes=True).then_inc(consts, 1)
                    pool.wait_ge(filled, 2)
                    pool.affine_select(out=ident[:], in_=ident[:], compare_op=ALU.not_equal, fill=1.0, base=0,
                                       pattern=[[-1, P]], channel_multiplier=1).then_inc(consts, 1)
                    pool.affine_select(out=below[:], in_=below[:], compare_op=ALU.is_gt, fill=0.0, base=0,
                                       pattern=[[-1, P]], channel_multiplier=1).then_inc(consts, 1)

                @block.vector
                def _(dve):
                    dve.memset(lh[:], 0.0)
                    dve.wait_ge(loaded, 16 * NG)
                    dve.tensor_copy(dst_col[:], dst_int[:].rearrange("p c j -> p (c j)"))
                    dve.tensor_reduce(low[:], dst_int[:], AX, ALU.min).then_inc(minmax, 1)
                    dve.tensor_reduce(high[:], dst_int[:], AX, ALU.max).then_inc(minmax, 1)
                    for g in range(NG):
                        for k, op in enumerate((ALU.min, ALU.max)):
                            dve.wait_ge(turned, 2 * g + k + 1)
                            dve.tensor_reduce(lh[0:RG, g, k:k + 1], ps[k][0:RG, 0:P], AX,
                                              op).then_inc(reduced, 1)
                    dve.wait_ge(reduced, 2 * NG)
                    dve.tensor_copy(lh_int[:], lh[:]).then_inc(as_int, 1)
                    dve.wait_ge(as_int, 1)
                    dve.tensor_single_scalar(lh_int[:], lh_int[:], P.bit_length() - 1,
                                             ALU.arith_shift_right).then_inc(as_int, 1)

                @block.tensor
                def _(pe):
                    pe.wait_ge(consts, 5)
                    pe.wait_ge(minmax, 2)
                    for g in range(NG):
                        for k, v in enumerate((low, high)):
                            if g:
                                pe.wait_ge(reduced, 2 * (g - 1) + k + 1)
                            pe.transpose(ps[k][0:RG, 0:P], v[:, g * RG:(g + 1) * RG],
                                         ident[:]).then_inc(turned, 1)

        with ExitStack() as layer0:
            s_src = sbuf(layer0, "s_src", [P, CH * TPC])
            s_max = sbuf(layer0, "s_max", [P, NB])
            att = sbuf(layer0, "att", [P, NB, 2])
            w_att = sbuf(layer0, "w_att", [P, 2 * D])
            with ExitStack() as ctx:
                idx = sbuf(ctx, "idx_a", [P, RING, TPC], I32)
                rows = sbuf(ctx, "rows_a", [P, RING, TPC, D])
                dst_row = sbuf(ctx, "dst_row_a", [P, RING, CE], I32)
                src_row = sbuf(ctx, "src_row_a", [P, RING, CE], I32)
                xw = sbuf(ctx, "xw", [P, 2, TPC, D])
                s_col = sbuf(ctx, "s_col", [P, RING, TPC])
                mask = sbuf(ctx, "mask", [P, CE])
                masked = sbuf(ctx, "masked", [P, CE])
                top_s = sbuf(ctx, "top_s", [P, 2])
                same = sbuf(ctx, "same_a", [P, TPC, P])
                repeats = sbuf(ctx, "repeats", [P, 2, TPC])
                away = sbuf(ctx, "away", [P, 2, TPC])
                ps = [psum(ctx, f"ps_s{k}", CE) for k in range(2)]
                w_loaded = sem(ctx, "w_loaded")
                idx_in, rows_in, src_in, kept = (sems(ctx, n) for n in ("a_idx_in", "a_rows_in", "a_src_in", "a_kept"))
                ready, used, weighed, logit = (sem(ctx, n) for n in ("a_ready", "a_used", "a_weighed", "a_logit"))
                spread, masked_ok, max_ok, folded = (sem(ctx, n) for n in ("a_spread", "a_masked", "a_max", "a_folded"))
                paired, before, counted, moved = (sem(ctx, n) for n in ("a_paired", "a_before", "a_counted", "a_moved"))
                extra, tick = sem(ctx, "a_extra"), sem(ctx, "a_tick")
                with nc.Block() as block:
                    @block.sync
                    def _(sp):
                        sp.dma_start(w_att[:], t["L0_gnn_attn_w"].partition_broadcast(P)).then_inc(w_loaded, 16)

                        def load(i, r, reused):
                            c = i * RING + r
                            if reused:
                                sp.wait_ge(used, c - RING + 1)
                                went_on(sp, sp_went_on)
                                sp.wait_ge(kept[r], i * 16)
                                went_on(sp, sp_went_on)
                            sp.dma_start(idx[:, r, :], src_chunks[c]).then_inc(idx_in[r], 16)
                            sp.dma_start(dst_row[:, r, :], dst_rows[c].to_broadcast([P, CE])).then_inc(src_in[r], 16)
                            sp.dma_start(src_row[:, r, :], src_rows[c].to_broadcast([P, CE])).then_inc(src_in[r], 16)

                        for r in range(RING):
                            load(0, r, False)
                        with sp.Fori(1, IT) as i:
                            for r in range(RING):
                                load(i, r, True)
                        for r in range(RING):
                            sp.wait_ge(kept[r], 16 * IT)

                    @block.gpsimd
                    def _(pool):
                        with pool.Fori(0, IT) as i:
                            for r in range(RING):
                                pool.wait_ge(idx_in[r], i * 16 + 16)
                                pool.sem_inc(tick, 1)
                                for j in range(TPC):
                                    pool.indirect_dma_start(
                                        rows[:, r, j, :], None, t["x"],
                                        bass.IndirectOffsetOnAxis(ap=idx[:, r, j:j + 1], axis=0)).then_inc(rows_in[r], 16)

                    @block.scalar
                    def _(act):
                        with act.Fori(0, IT) as i:
                            for r in range(RING):
                                act.wait_ge(rows_in[r], i * (16 * TPC) + 16 * TPC)
                                act.dma_start(x_gathered[i * RING + r],
                                              rows[:, r, :, :].rearrange("p j f -> p (j f)")).then_inc(kept[r], 16)

                    @block.tensor
                    def _(pe):
                        with pe.Fori(0, IT) as i:
                            for r in range(RING):
                                c = i * RING + r
                                pe.wait_ge(logit, c + 1)
                                pe.wait_ge(folded, c + 1)
                                for j in range(TPC):
                                    last = pe.matmul(ps[r % 2][:, j * P:(j + 1) * P],
                                                     s_col[:, r, j:j + 1].to_broadcast([P, P]), ident[:],
                                                     start=True, stop=True)
                                last.then_inc(spread, 1)

                    @block.vector
                    def _(dve):
                        regs = [dve.alloc_register("a_first"), dve.alloc_register("a_last")]
                        n_extra = dve.alloc_register("a_extras")
                        dve.reg_mov(n_extra, 0)
                        dve.sem_inc(folded, 2)
                        dve.memset(s_max[:], -BIG).then_inc(ready, 1)
                        dve.wait_ge(ready, 1)
                        dve.wait_ge(w_loaded, 16)

                        def largest(r, b, sem_, count):
                            row = dst_row[:, r, :].rearrange("n (p j) -> n j p", j=TPC)
                            dve.tensor_scalar(mask[:].rearrange("n (j p) -> n j p", j=TPC), row,
                                              node_id[:, bass.ds(b, 1)], -BIG,
                                              ALU.not_equal, ALU.mult).then_inc(sem_[0], 1)
                            dve.wait_ge(sem_[0], count())
                            went_on(dve, dve_went_on)
                            dve.tensor_tensor_reduce(out=masked[:], in0=ps[r % 2][:], in1=mask[:], scale=1.0,
                                                     scalar=-BIG, op0=ALU.add, op1=ALU.max,
                                                     accum_out=top_s[:, 0:1]).then_inc(sem_[1], 1)
                            dve.wait_ge(sem_[1], count())
                            m = s_max[:, bass.ds(b, 1)]
                            return dve.tensor_tensor(m, m, top_s[:, 0:1], ALU.max)

                        with dve.Fori(0, IT) as i:
                            for r in range(RING):
                                c = i * RING + r
                                dve.wait_ge(rows_in[r], i * (16 * TPC) + 16 * TPC)
                                dve.tensor_tensor(xw[:, r % 2, :, :], rows[:, r, :, :],
                                                  w_att[:, 0:D].unsqueeze(1).to_broadcast([P, TPC, D]),
                                                  ALU.mult).then_inc(weighed, 1)
                                dve.wait_ge(weighed, c + 1)
                                dve.tensor_reduce(s_col[:, r, :], xw[:, r % 2, :, :], AX, ALU.add).then_inc(logit, 1)
                                dve.wait_ge(src_in[r], i * 32 + 32)
                                same_src(same[:], src_row[:, r, :], idx[:, r, :]).then_inc(paired, 1)
                                dve.tensor_tensor(away[:, r % 2, :], dump_id[:].to_broadcast([P, TPC]), idx[:, r, :],
                                                  ALU.subtract)
                                dve.wait_ge(logit, c + 1)
                                dve.tensor_copy(cols(s_src, c, TPC), s_col[:, r, :])
                                dve.wait_ge(paired, c + 1)
                                dve.tensor_tensor(same[:], same[:], below[:].unsqueeze(1).to_broadcast([P, TPC, P]),
                                                  ALU.mult).then_inc(before, 1)
                                dve.wait_ge(before, c + 1)
                                dve.tensor_reduce(repeats[:, r % 2, :], same[:], AX, ALU.add).then_inc(counted, 1)
                                dve.wait_ge(counted, c + 1)
                                dve.scalar_tensor_tensor(out=away[:, r % 2, :], in0=repeats[:, r % 2, :], scalar=1.0,
                                                         in1=away[:, r % 2, :], op0=ALU.min,
                                                         op1=ALU.mult).then_inc(moved, 1)
                                dve.wait_ge(moved, c + 1)
                                dve.tensor_tensor(cols(uniq, c, TPC), away[:, r % 2, :], idx[:, r, :], ALU.add)
                                first, last = block_range(dve, regs, c)
                                dve.wait_ge(spread, c + 1)
                                largest(r, first, (masked_ok, max_ok), lambda: c + 1).then_inc(ready, 1)
                                went_on(dve, dve_went_on)
                                with dve.If_lt(regs[0], regs[1]):
                                    with dve.Fori(first + 1, last + 1) as b:
                                        def one_more():
                                            dve.reg_add(n_extra, n_extra, 1)
                                            return dve.snap(n_extra)

                                        largest(r, b, (extra, extra), one_more).then_inc(extra, 1)
                                        dve.wait_ge(extra, one_more())
                                dve.wait_ge(ready, c + 2)
                                dve.sem_inc(folded, 1)
                                dve.sem_inc(used, 1)

            with ExitStack() as ctx:
                xw = sbuf(ctx, "xw_n", [P, NB, D])
                lin = sbuf(ctx, "lin", [P, NB])
                step = sem(ctx, "att_step")
                with nc.Block() as block:
                    @block.vector
                    def _(dve):
                        dve.tensor_tensor(xw[:], X[:], w_att[:, D:2 * D].unsqueeze(1).to_broadcast([P, NB, D]),
                                          ALU.mult).then_inc(step, 1)
                        dve.memset(acc[:], 0.0)
                        dve.wait_ge(step, 1)
                        dve.tensor_reduce(att[:, :, 0], xw[:], AX, ALU.add).then_inc(step, 1)
                        dve.wait_ge(step, 2)
                        dve.tensor_tensor(lin[:], s_max[:], att[:, :, 0], ALU.add).then_inc(step, 1)
                        dve.wait_ge(step, 3)
                        dve.scalar_tensor_tensor(out=att[:, :, 1], in0=lin[:], scalar=SLOPE, in1=lin[:],
                                                 op0=ALU.mult, op1=ALU.max)

            with ExitStack() as ctx:
                rows = sbuf(ctx, "rows_b", [P, RING, TPC, D])
                dst_row = sbuf(ctx, "dst_row_b", [P, RING, CE], I32)
                onT = sbuf(ctx, "onT_b", [P, 2, CE])
                on = sbuf(ctx, "on_b", [P, 2, TPC, P])
                lin = sbuf(ctx, "lin_b", [P, 2, TPC])
                logits = sbuf(ctx, "logits", [P, 2, TPC])
                shifted = sbuf(ctx, "shifted", [P, 2, TPC])
                H = sbuf(ctx, "H_b", [P, 2, TPC, D + 1])
                ps_g = [psum(ctx, f"ps_gb{k}", 512) for k in range(2)]
                ps_s = [psum(ctx, f"ps_sb{k}", 512) for k in range(2)]
                ps_x = psum(ctx, "ps_xb", 512)
                rows_in = sems(ctx, "b_rows_in")
                names = ("b_used", "b_onT", "b_on", "b_got", "b_lin", "b_logit", "b_shift", "b_exp", "b_H",
                         "b_sum", "b_added", "b_xr", "b_xd", "b_xa")
                used, onT_ok, on_ok, got, lin_ok, logit_ok, shift_ok, exp_ok, H_ok, summed, added, x_ready, x_done, \
                    x_added = (sem(ctx, n) for n in names)
                with nc.Block() as block:
                    @block.sync
                    def _(sp):
                        with sp.Fori(0, IT) as i:
                            for r in range(RING):
                                c = i * RING + r
                                sp.wait_ge(used, c + 1)
                                went_on(sp, sp_went_on)
                                sp.dma_start(rows[:, r, :, :].rearrange("p j f -> p (j f)"),
                                             x_gathered[c]).then_inc(rows_in[r], 16)
                                sp.dma_start(dst_row[:, r, :],
                                             dst_rows[c].to_broadcast([P, CE])).then_inc(rows_in[r], 16)

                    @block.scalar
                    def _(act):
                        with act.Fori(0, IT) as i:
                            for r in range(RING):
                                act.wait_ge(shift_ok, i * RING + r + 1)
                                act.activation(H[:, r % 2, :, D], shifted[:, r % 2, :], ACT.Exp).then_inc(exp_ok, 1)

                    @block.tensor
                    def _(pe):
                        regs = [pe.alloc_register("b_first"), pe.alloc_register("b_last")]
                        n_extra = pe.alloc_register("b_extras")
                        pe.reg_mov(n_extra, 0)

                        def read(r, b, start):
                            for j in range(TPC):
                                last = pe.matmul(ps_g[r % 2][:, 2 * j:2 * j + 2], onT[:, r % 2, j * P:(j + 1) * P],
                                                 att[:, bass.ds(b, 1), :].rearrange("p o f -> p (o f)"),
                                                 start=start and j == 0, stop=True, skip_group_check=True)
                            return last

                        def add_up(out, r):
                            for j in range(TPC):
                                last = pe.matmul(out[:, 0:D + 1], on[:, r % 2, j, :], H[:, r % 2, j, :],
                                                 start=j == 0, stop=j == TPC - 1)
                            return last

                        with pe.Fori(0, IT) as i:
                            for r in range(RING):
                                c = i * RING + r
                                first, last = block_range(pe, regs, c)
                                pe.wait_ge(onT_ok, c + 1)
                                read(r, first, True).then_inc(got, 1)
                                with pe.If_lt(regs[0], regs[1]):
                                    with pe.Fori(first + 1, last + 1) as b:
                                        pe.reg_add(n_extra, n_extra, 1)
                                        k = pe.snap(n_extra)
                                        pe.wait_ge(x_ready, k)
                                        read(r, b, False).then_inc(x_done, 1)
                                pe.wait_ge(on_ok, c + 1)
                                pe.wait_ge(H_ok, c + 1)
                                add_up(ps_s[r % 2], r).then_inc(summed, 1)
                                with pe.If_lt(regs[0], regs[1]):
                                    with pe.Fori(first + 1, last + 1) as b:
                                        pe.reg_add(n_extra, n_extra, 1)
                                        k = pe.snap(n_extra)
                                        pe.wait_ge(x_ready, k)
                                        add_up(ps_x, r).then_inc(x_done, 1)

                    @block.vector
                    def _(dve):
                        regs = [dve.alloc_register("bv_first"), dve.alloc_register("bv_last")]
                        n_extra = dve.alloc_register("bv_extras")
                        n_added = dve.alloc_register("bv_added")
                        dve.reg_mov(n_extra, 0)
                        dve.reg_mov(n_added, 0)
                        dve.sem_inc(used, RING)
                        with dve.Fori(0, IT) as i:
                            for r in range(RING):
                                c = i * RING + r
                                first, last = block_range(dve, regs, c)
                                dve.wait_ge(rows_in[r], i * 32 + 32)
                                one_hot_T(onT[:, r % 2, :], dst_row[:, r, :], first).then_inc(onT_ok, 1)
                                one_hot(on[:, r % 2, :, :], c, first).then_inc(on_ok, 1)
                                dve.wait_ge(got, c + 1)
                                went_on(dve, dve_went_on)
                                with dve.If_lt(regs[0], regs[1]):
                                    with dve.Fori(first + 1, last + 1) as b:
                                        dve.reg_add(n_extra, n_extra, 1)
                                        k = dve.snap(n_extra)
                                        one_hot_T(onT[:, r % 2, :], dst_row[:, r, :], b).then_inc(x_ready, 1)
                                        dve.wait_ge(x_done, k)
                                pair = ps_g[r % 2][:, 0:2 * TPC].rearrange("p (j k) -> p j k", k=2)
                                dve.tensor_tensor(lin[:, r % 2, :], pair[:, :, 0], cols(s_src, c, TPC),
                                                  ALU.add).then_inc(lin_ok, 1)
                                dve.wait_ge(lin_ok, c + 1)
                                dve.scalar_tensor_tensor(out=logits[:, r % 2, :], in0=lin[:, r % 2, :], scalar=SLOPE,
                                                         in1=lin[:, r % 2, :], op0=ALU.mult,
                                                         op1=ALU.max).then_inc(logit_ok, 1)
                                dve.wait_ge(logit_ok, c + 1)
                                dve.tensor_tensor(shifted[:, r % 2, :], logits[:, r % 2, :], pair[:, :, 1],
                                                  ALU.subtract).then_inc(shift_ok, 1)
                                dve.wait_ge(exp_ok, c + 1)
                                dve.tensor_tensor(H[:, r % 2, :, 0:D], rows[:, r, :, :],
                                                  H[:, r % 2, :, D:D + 1].to_broadcast([P, TPC, D]),
                                                  ALU.mult).then_inc(H_ok, 1)
                                dve.wait_ge(summed, c + 1)
                                add_to_block(first, D + 1, ps_s[r % 2][:, 0:D + 1]).then_inc(added, 1)
                                went_on(dve, dve_went_on)
                                with dve.If_lt(regs[0], regs[1]):
                                    with dve.Fori(first + 1, last + 1) as b:
                                        dve.reg_add(n_extra, n_extra, 1)
                                        dve.reg_add(n_added, n_added, 1)
                                        k = dve.snap(n_extra)
                                        one_hot(on[:, r % 2, :, :], c, b).then_inc(x_ready, 1)
                                        dve.wait_ge(x_done, k)
                                        add_to_block(b, D + 1, ps_x[:, 0:D + 1]).then_inc(x_added, 1)
                                        dve.wait_ge(x_added, dve.snap(n_added))
                                dve.wait_ge(added, c + 1)
                                dve.sem_inc(used, 1)

        def layernorm_dve(dve, tmp, small, step, v, root_ok, root_from):
            mean, var = small[:, 0, :], small[:, 1, :]
            dve.tensor_reduce(mean, X[:], AX, ALU.add).then_inc(step, 1)
            dve.wait_ge(step, v + 1)
            dve.tensor_scalar(mean, mean, 1.0 / D, None, ALU.mult).then_inc(step, 1)
            dve.wait_ge(step, v + 2)
            dve.tensor_tensor(X[:], X[:], mean.unsqueeze(2).to_broadcast([P, NB, D]), ALU.subtract).then_inc(step, 1)
            dve.wait_ge(step, v + 3)
            dve.tensor_tensor(tmp, X[:], X[:], ALU.mult).then_inc(step, 1)
            dve.wait_ge(step, v + 4)
            dve.tensor_reduce(var, tmp, AX, ALU.add).then_inc(step, 1)
            dve.wait_ge(step, v + 5)
            dve.tensor_scalar(var, var, 1.0 / D, EPS, ALU.mult, ALU.add).then_inc(root_from, 1)
            dve.wait_ge(root_ok, 1)
            dve.reciprocal(var, var).then_inc(step, 1)
            dve.wait_ge(step, v + 6)
            dve.tensor_tensor(X[:], X[:], var.unsqueeze(2).to_broadcast([P, NB, D]), ALU.mult).then_inc(step, 1)
            dve.wait_ge(step, v + 7)

        def layernorm_act(act, small, root_ok, root_from):
            act.wait_ge(root_from, 1)
            act.activation(small[:, 1, :], small[:, 1, :], ACT.Sqrt).then_inc(root_ok, 1)

        def turn(pe, out, rows, width):
            for q in range(GB):
                last = pe.transpose(out[0:width, q * P:(q + 1) * P], rows[:, q, :], ident[:])
            return last

        layer1 = top.enter_context(ExitStack())
        flow_dst = sbuf(layer1, "flow_dst", [P, NB, 2 * FH])
        with ExitStack() as ctx:
            tmp = sbuf(ctx, "tmp0", [P, NB, D])
            small = sbuf(ctx, "small0", [P, 2, NB])
            w_ab = sbuf(ctx, "w_ab", [D, 2 * FH])
            zero = sbuf(ctx, "zero", [P, NP // P * HW + HW])
            xs = sbuf(ctx, "xs0", [P, GB, D])
            xT = sbuf(ctx, "xT0", [D, GB * P])
            swapped = sbuf(ctx, "swapped", [P, GB, 2 * FH])
            ps_t = psum(ctx, "ps_t0", 1024)
            ps_m = psum(ctx, "ps_m0", 1024)
            names = ("n0_step", "n0_rf", "n0_ro", "n0_w", "n0_z", "n0_zeroed", "n0_xs", "n0_t", "n0_xT", "n0_m",
                     "n0_d", "n0_sw", "n0_st")
            step, root_from, root_ok, w_in, zero_ok, zeroed, xs_ok, t_ok, xT_ok, m_ok, d_ok, sw_ok, stored = \
                (sem(ctx, n) for n in names)
            with nc.Block() as block:
                @block.sync
                def _(sp):
                    sp.dma_start(w_ab[:, 0:FH], t["L1_gnn_Wf1"][0:D, :]).then_inc(w_in, 16)
                    sp.dma_start(w_ab[:, FH:2 * FH], t["L1_gnn_Wf1"][D:2 * D, :]).then_inc(w_in, 16)
                    sp.wait_ge(zero_ok, 1)
                    for j in range(TPC):
                        sp.dma_start(flow_sums[j].rearrange("(p b) f -> p (b f)", p=P),
                                     zero[:, 0:TR // P * HW]).then_inc(zeroed, 16)
                        sp.dma_start(spline_sums[j].rearrange("(p b) f -> p (b f)", p=P),
                                     zero[:, 0:TR // P * D]).then_inc(zeroed, 16)
                    with sp.Fori(0, NS) as k:
                        sp.wait_ge(sw_ok, k + 1)
                        sp.dma_start(flow_rows[bass.ds(k * (GB * P), GB * P), :].rearrange("(q p) f -> p q f", p=P),
                                     swapped[:]).then_inc(stored, 16)
                    sp.wait_ge(stored, 16 * NS)
                    sp.wait_ge(zeroed, 32 * TPC)

                @block.scalar
                def _(act):
                    layernorm_act(act, small, root_ok, root_from)

                    def swap(k, reused):
                        act.wait_ge(d_ok, k + 1)
                        if reused:
                            act.wait_ge(stored, k * 16)
                        m = flow_dst[:, bass.ds(k * GB, GB), :].rearrange("p q (h f) -> p q h f", h=2)
                        s = swapped[:].rearrange("p q (h f) -> p q h f", h=2)
                        act.copy(s[:, :, 0, :], m[:, :, 1, :])
                        act.copy(s[:, :, 1, :], m[:, :, 0, :]).then_inc(sw_ok, 1)

                    swap(0, False)
                    with act.Fori(1, NS) as k:
                        swap(k, True)

                @block.tensor
                def _(pe):
                    pe.wait_ge(w_in, 32)
                    with pe.Fori(0, NS) as k:
                        pe.wait_ge(xs_ok, k + 1)
                        turn(pe, ps_t, xs, D).then_inc(t_ok, 1)
                        pe.wait_ge(xT_ok, k + 1)
                        for q in range(GB):
                            last = pe.matmul(ps_m[:, q * P:(q + 1) * P], xT[:, q * P:(q + 1) * P], w_ab[:],
                                             start=True, stop=True)
                        last.then_inc(m_ok, 1)

                @block.vector
                def _(dve):
                    dve.memset(zero[:], 0.0).then_inc(zero_ok, 1)
                    dve.tensor_scalar(small[:, 0, :], acc[:, :, D], 1e-30, None, ALU.max).then_inc(step, 1)
                    dve.wait_ge(step, 1)
                    dve.reciprocal(small[:, 1, :], small[:, 0, :]).then_inc(step, 1)
                    dve.wait_ge(step, 2)
                    dve.tensor_tensor(tmp[:], acc[:, :, 0:D], small[:, 1, :].unsqueeze(2).to_broadcast([P, NB, D]),
                                      ALU.mult).then_inc(step, 1)
                    dve.wait_ge(step, 3)
                    dve.tensor_tensor(X[:], X[:], tmp[:], ALU.add).then_inc(step, 1)
                    dve.wait_ge(step, 4)
                    layernorm_dve(dve, tmp[:], small, step, 4, root_ok, root_from)
                    dve.memset(acc[:], 0.0)
                    with dve.Fori(0, NS) as k:
                        dve.tensor_copy(xs[:], X[:, bass.ds(k * GB, GB), :]).then_inc(xs_ok, 1)
                        dve.wait_ge(t_ok, k + 1)
                        dve.tensor_copy(xT[:], ps_t[0:D, 0:GB * P]).then_inc(xT_ok, 1)
                        dve.wait_ge(m_ok, k + 1)
                        dve.tensor_copy(flow_dst[:, bass.ds(k * GB, GB), :],
                                        ps_m[:, 0:GB * 2 * FH].rearrange("p (q f) -> p q f", f=2 * FH)).then_inc(d_ok, 1)

        clear_semaphores()

        with ExitStack() as ctx:
            idx = sbuf(ctx, "idx_1", [P, RING, TPC], I32)
            uniq_idx = sbuf(ctx, "uniq_1", [P, RING, TPC], I32)
            rows = sbuf(ctx, "rows_1", [P, RING, TPC * 2 * FH])
            dst_row = sbuf(ctx, "dst_row_1", [P, RING, CE], I32)
            src_row = sbuf(ctx, "src_row_1", [P, RING, CE], I32)
            attr = sbuf(ctx, "attr", [P, RING, TPC * EA + 1])
            attrT = sbuf(ctx, "attrT", [TPC * EA + 1, 2, P])
            w_c = sbuf(ctx, "w_c", [TPC * EA + 1, TPC, 2, FH])
            onT = sbuf(ctx, "onT_1", [P, 2, CE])
            on = sbuf(ctx, "on_1", [P, 2, TPC, P])
            same = sbuf(ctx, "same_1", [P, 2, TPC, P])
            H = sbuf(ctx, "H_1", [P, 2, TPC, 2, HW])
            back = sbuf(ctx, "back_1", [P, RING, TPC, HW])
            ps_h = [psum(ctx, f"ps_h{k}", CE) for k in range(2)]
            ps_t = psum(ctx, "ps_t1", 512)
            ps_s = [psum(ctx, f"ps_s1{k}", 512) for k in range(2)]
            ps_d = [psum(ctx, f"ps_d1{k}", 512) for k in range(2)]
            ps_x = psum(ctx, "ps_x1", 512)
            idx_in, rows_in, edges_in, uniq_in = (sems(ctx, n) for n in ("f_idx", "f_rows", "f_edges", "f_uniq"))
            scattered = sems(ctx, "f_scattered", TPC)
            names = ("f_w0", "f_w", "f_onT", "f_on", "f_same", "f_got", "f_turned", "f_attrT", "f_pre", "f_H", "f_sum",
                     "f_dsum", "f_back", "f_added", "f_xr", "f_xd", "f_xa", "f_tick", "f_done", "f_ones")
            w_zero, w_in, onT_ok, on_ok, same_ok, got, turned, attrT_ok, pre_ok, H_ok, summed, dsummed, back_ok, \
                added, x_ready, x_done, x_added, tick, done, ones_ok = (sem(ctx, n) for n in names)
            with nc.Block() as block:
                @block.sync
                def _(sp):
                    sp.wait_ge(w_zero, 1)
                    for j in range(TPC):
                        for h in range(2):
                            sp.dma_start(w_c[j * EA:(j + 1) * EA, j, h, :],
                                         t["L1_gnn_Wf1"][2 * D:, :]).then_inc(w_in, 16)
                            sp.dma_start(w_c[TPC * EA:, j, h, :],
                                         t["L1_gnn_bf1"].unsqueeze(0)).then_inc(w_in, 16)
                    sp.wait_ge(ones_ok, 2)

                    def load(i, r, reused):
                        c = i * RING + r
                        if reused:
                            sp.wait_ge(done, c - RING + 1)
                            went_on(sp, sp_went_on)
                            sp.wait_ge(pre_ok, c - RING + 1)
                            went_on(sp, sp_went_on)
                        sp.dma_start(idx[:, r, :], src_chunks[c]).then_inc(idx_in[r], 16)
                        sp.dma_start(dst_row[:, r, :], dst_rows[c].to_broadcast([P, CE])).then_inc(edges_in[r], 16)
                        sp.dma_start(attr[:, r, 0:TPC * EA], attr_chunks[c]).then_inc(edges_in[r], 16)
                        sp.dma_start(src_row[:, r, :], src_rows[c].to_broadcast([P, CE])).then_inc(edges_in[r], 16)
                        if reused:
                            for j in range(TPC):
                                sp.wait_ge(scattered[j], (c - RING + 1) * 16)
                                went_on(sp, sp_went_on)
                        sp.dma_start(uniq_idx[:, r, :], cols(uniq, c, TPC)).then_inc(uniq_in[r], 16)

                    for r in range(RING):
                        load(0, r, False)
                    with sp.Fori(1, IT) as i:
                        for r in range(RING):
                            load(i, r, True)
                    for j in range(TPC):
                        sp.wait_ge(scattered[j], 16 * CH)

                @block.gpsimd
                def _(pool):
                    tables(pool, IT, idx_in, lambda r, j: rows[:, r, j * 2 * FH:(j + 1) * 2 * FH], flow_rows, idx,
                           rows_in, back_ok, uniq_in, scattered, flow_sums, uniq_idx, lambda r, j: back[:, r, j, :],
                           tick)

                @block.scalar
                def _(act):
                    with act.Fori(0, IT) as i:
                        for r in range(RING):
                            c = i * RING + r
                            act.wait_ge(turned, c + 1)
                            act.copy(attrT[:, r % 2, :], ps_t[0:TPC * EA + 1, 0:P]).then_inc(attrT_ok, 1)
                            act.wait_ge(pre_ok, c + 1)
                            act.activation(H[:, r % 2, :, :, 0:FH],
                                           ps_h[r % 2][:].rearrange("p (j h f) -> p j h f", j=TPC, h=2),
                                           ACT.Relu).then_inc(H_ok, 1)
                            act.wait_ge(dsummed, c + 1)
                            act.wait_ge(uniq_in[r], i * 16 + 16)
                            act.copy(back[:, r, :, :], ps_d[r % 2][:, 0:TPC * HW].rearrange("p (j f) -> p j f", j=TPC)
                                     ).then_inc(back_ok, 1)

                @block.tensor
                def _(pe):
                    regs = [pe.alloc_register("f_first"), pe.alloc_register("f_last")]
                    n_extra = pe.alloc_register("f_extras")
                    pe.reg_mov(n_extra, 0)
                    pe.wait_ge(w_in, 16 * 4 * TPC)

                    def read(r, b):
                        for j in range(TPC):
                            last = pe.matmul(ps_h[r % 2][:, j * P:(j + 1) * P], onT[:, r % 2, j * P:(j + 1) * P],
                                             flow_dst[:, bass.ds(b, 1), :].rearrange("p o f -> p (o f)"),
                                             start=False, stop=True, skip_group_check=True)
                        return last

                    def add_up(out, r):
                        for j in range(TPC):
                            last = pe.matmul(out[:, 0:HW], on[:, r % 2, j, :], H[:, r % 2, j, 0, :],
                                             start=j == 0, stop=j == TPC - 1)
                        return last

                    with pe.Fori(0, IT) as i:
                        for r in range(RING):
                            c = i * RING + r
                            first, last = block_range(pe, regs, c)
                            pe.wait_ge(edges_in[r], i * 48 + 48)
                            pe.transpose(ps_t[0:TPC * EA + 1, 0:P], attr[:, r, :], ident[:]).then_inc(turned, 1)
                            pe.wait_ge(attrT_ok, c + 1)
                            pe.matmul(ps_h[r % 2][:], attrT[:, r % 2, :], w_c[:].rearrange("k j h f -> k (j h f)"),
                                      start=True, stop=True, skip_group_check=True)
                            pe.wait_ge(onT_ok, c + 1)
                            read(r, first).then_inc(got, 1)
                            with pe.If_lt(regs[0], regs[1]):
                                with pe.Fori(first + 1, last + 1) as b:
                                    pe.reg_add(n_extra, n_extra, 1)
                                    k = pe.snap(n_extra)
                                    pe.wait_ge(x_ready, k)
                                    read(r, b).then_inc(x_done, 1)
                            pe.wait_ge(rows_in[r], i * (16 * TPC) + 16 * TPC)
                            pe.matmul(ps_h[r % 2][:], ident[:], rows[:, r, :],
                                      start=False, stop=True, skip_group_check=True).then_inc(pre_ok, 1)
                            pe.wait_ge(on_ok, c + 1)
                            pe.wait_ge(same_ok, c + 1)
                            pe.wait_ge(H_ok, c + 1)
                            add_up(ps_s[r % 2], r).then_inc(summed, 1)
                            for j in range(TPC):
                                last_mm = pe.matmul(ps_d[r % 2][:, j * HW:(j + 1) * HW], same[:, r % 2, j, :],
                                                    H[:, r % 2, j, 1, :], start=True, stop=True)
                            last_mm.then_inc(dsummed, 1)
                            with pe.If_lt(regs[0], regs[1]):
                                with pe.Fori(first + 1, last + 1) as b:
                                    pe.reg_add(n_extra, n_extra, 1)
                                    k = pe.snap(n_extra)
                                    pe.wait_ge(x_ready, k)
                                    add_up(ps_x, r).then_inc(x_done, 1)

                @block.vector
                def _(dve):
                    dve.memset(w_c[:], 0.0).then_inc(w_zero, 1)
                    dve.memset(attr[:], 1.0).then_inc(ones_ok, 1)
                    dve.memset(H[:], 1.0).then_inc(ones_ok, 1)
                    regs = [dve.alloc_register("fv_first"), dve.alloc_register("fv_last")]
                    n_extra = dve.alloc_register("fv_extras")
                    n_added = dve.alloc_register("fv_added")
                    dve.reg_mov(n_extra, 0)
                    dve.reg_mov(n_added, 0)
                    with dve.Fori(0, IT) as i:
                        for r in range(RING):
                            c = i * RING + r
                            first, last = block_range(dve, regs, c)
                            dve.wait_ge(edges_in[r], i * 48 + 48)
                            one_hot_T(onT[:, r % 2, :], dst_row[:, r, :], first).then_inc(onT_ok, 1)
                            one_hot(on[:, r % 2, :, :], c, first).then_inc(on_ok, 1)
                            dve.wait_ge(idx_in[r], i * 16 + 16)
                            same_src(same[:, r % 2, :, :], src_row[:, r, :], idx[:, r, :]).then_inc(same_ok, 1)
                            dve.wait_ge(got, c + 1)
                            went_on(dve, dve_went_on)
                            with dve.If_lt(regs[0], regs[1]):
                                with dve.Fori(first + 1, last + 1) as b:
                                    dve.reg_add(n_extra, n_extra, 1)
                                    k = dve.snap(n_extra)
                                    one_hot_T(onT[:, r % 2, :], dst_row[:, r, :], b).then_inc(x_ready, 1)
                                    dve.wait_ge(x_done, k)
                            dve.wait_ge(summed, c + 1)
                            add_to_block(first, HW, ps_s[r % 2][:, 0:HW]).then_inc(added, 1)
                            dve.wait_ge(dsummed, c + 1)
                            went_on(dve, dve_went_on)
                            with dve.If_lt(regs[0], regs[1]):
                                with dve.Fori(first + 1, last + 1) as b:
                                    dve.reg_add(n_extra, n_extra, 1)
                                    dve.reg_add(n_added, n_added, 1)
                                    k = dve.snap(n_extra)
                                    one_hot(on[:, r % 2, :, :], c, b).then_inc(x_ready, 1)
                                    dve.wait_ge(x_done, k)
                                    add_to_block(b, HW, ps_x[:, 0:HW]).then_inc(x_added, 1)
                                    dve.wait_ge(x_added, dve.snap(n_added))
                            dve.wait_ge(added, c + 1)
                            dve.sem_inc(done, 1)
        layer1.close()

        with ExitStack() as ctx:
            tmp = sbuf(ctx, "tmp1", [P, NB, D])
            small = sbuf(ctx, "small1", [P, 2, NB])
            part = sbuf(ctx, "part1", [P, 2, NB, HW])
            w_f2 = sbuf(ctx, "w_f2", [HW, FH])
            w_n1 = sbuf(ctx, "w_n1", [FH, FH])
            b_n1 = sbuf(ctx, "b_n1", [FH, 1])
            w_n2 = sbuf(ctx, "w_n2", [HW, D])
            hs = sbuf(ctx, "hs", [P, GB, HW])
            hT = sbuf(ctx, "hT", [HW, GB * P])
            fT = sbuf(ctx, "fT", [FH, GB * P])
            zT = sbuf(ctx, "zT", [HW, GB * P])
            ps_t = psum(ctx, "ps_t2", 1024)
            ps_f = psum(ctx, "ps_f2", 1024)
            ps_m = psum(ctx, "ps_m2", 512)
            names = ("n1_step", "n1_rf", "n1_ro", "n1_w", "n1_sum", "n1_hs", "n1_t", "n1_hT", "n1_f", "n1_fT",
                     "n1_z", "n1_zT", "n1_m", "n1_x", "n1_one")
            step, root_from, root_ok, w_in, part_sum, hs_ok, t_ok, hT_ok, f_ok, fT_ok, z_ok, zT_ok, m_ok, x_ok, \
                one_ok = (sem(ctx, n) for n in names)
            part_in = sems(ctx, "n1_part", 2)
            deg_ok = sem(ctx, "n1_deg")
            halves = ((0, 512), (512, GB * P))
            with nc.Block() as block:
                @block.sync
                def _(sp):
                    for dst, src in ((w_f2[0:FH, :], t["L1_gnn_Wf2"]), (w_f2[FH:, :], t["L1_gnn_bf2"].unsqueeze(0)),
                                     (w_n1[:], t["L1_gnn_Wn1"]), (b_n1[:], t["L1_gnn_bn1"].unsqueeze(1)),
                                     (w_n2[0:FH, :], t["L1_gnn_Wn2"]), (w_n2[FH:, :], t["L1_gnn_bn2"].unsqueeze(0))):
                        sp.dma_start(dst, src).then_inc(w_in, 16)
                    for j in range(TPC):
                        if j >= 2:
                            sp.wait_ge(part_sum, 2 * (j - 2) + 2)
                        sp.dma_start(part[:, j % 2, :, :], flow_sums[j][0:NP, :].rearrange("(b p) f -> p b f", p=P)
                                     ).then_inc(part_in[j % 2], 16)

                @block.scalar
                def _(act):
                    act.wait_ge(w_in, 96)
                    with act.Fori(0, NS) as k:
                        act.wait_ge(f_ok, k + 1)
                        act.copy(fT[:], ps_f[0:FH, 0:GB * P]).then_inc(fT_ok, 1)
                        act.wait_ge(z_ok, k + 1)
                        act.activation(zT[0:FH, :], ps_f[0:FH, 0:GB * P], ACT.Relu, bias=b_n1[:]).then_inc(zT_ok, 1)
                    layernorm_act(act, small, root_ok, root_from)

                @block.tensor
                def _(pe):
                    pe.wait_ge(w_in, 96)
                    pe.wait_ge(one_ok, 1)
                    with pe.Fori(0, NS) as k:
                        pe.wait_ge(hs_ok, k + 1)
                        turn(pe, ps_t, hs, HW).then_inc(t_ok, 1)
                        pe.wait_ge(hT_ok, k + 1)
                        for a, z in halves:
                            last = pe.matmul(ps_f[0:FH, a:z], w_f2[:], hT[:, a:z], start=True, stop=True)
                        last.then_inc(f_ok, 1)
                        pe.wait_ge(fT_ok, k + 1)
                        went_on(pe, pe_went_on)
                        for a, z in halves:
                            last = pe.matmul(ps_f[0:FH, a:z], w_n1[:], fT[:, a:z], start=True, stop=True)
                        last.then_inc(z_ok, 1)
                        pe.wait_ge(zT_ok, k + 1)
                        for q in range(GB):
                            last = pe.matmul(ps_m[:, q * D:(q + 1) * D], zT[:, q * P:(q + 1) * P], w_n2[:],
                                             start=True, stop=True)
                        last.then_inc(m_ok, 1)

                @block.vector
                def _(dve):
                    dve.memset(zT[FH:HW, :], 1.0).then_inc(one_ok, 1)
                    dve.tensor_copy(deg_dst[:], acc[:, :, FH]).then_inc(deg_ok, 1)
                    dve.wait_ge(deg_ok, 1)
                    for j in range(TPC):
                        dve.wait_ge(part_in[j % 2], 16 * (j // 2 + 1))
                        if j:
                            dve.wait_ge(part_sum, 2 * j)
                            dve.tensor_tensor(deg_src[:], deg_src[:], part[:, j % 2, :, FH], ALU.add).then_inc(part_sum, 1)
                        else:
                            dve.tensor_copy(deg_src[:], part[:, 0, :, FH]).then_inc(part_sum, 1)
                        dve.tensor_tensor(acc[:], acc[:], part[:, j % 2, :, :], ALU.add).then_inc(part_sum, 1)
                    dve.wait_ge(part_sum, 2 * TPC)
                    with dve.Fori(0, NS) as k:
                        dve.tensor_copy(hs[:], acc[:, bass.ds(k * GB, GB), :]).then_inc(hs_ok, 1)
                        dve.wait_ge(t_ok, k + 1)
                        dve.tensor_copy(hT[:], ps_t[0:HW, 0:GB * P]).then_inc(hT_ok, 1)
                        dve.wait_ge(m_ok, k + 1)
                        xb = X[:, bass.ds(k * GB, GB), :]
                        dve.tensor_tensor(xb, xb, ps_m[:, 0:GB * D].rearrange("p (q f) -> p q f", f=D),
                                          ALU.add).then_inc(x_ok, 1)
                    dve.wait_ge(x_ok, NS)
                    layernorm_dve(dve, tmp[:], small, step, 0, root_ok, root_from)
                    dve.memset(acc[:], 0.0)

        clear_semaphores()

        with ExitStack() as ctx:
            idx = sbuf(ctx, "idx_2", [P, RING, TPC], I32)
            uniq_idx = sbuf(ctx, "uniq_2", [P, RING, TPC], I32)
            dst_row = sbuf(ctx, "dst_row_2", [P, RING, CE], I32)
            src_row = sbuf(ctx, "src_row_2", [P, RING, CE], I32)
            pseudo = sbuf(ctx, "pseudo", [P, 2, RING * TPC, 2])
            knots = sbuf(ctx, "knots", [P, KS])
            place = sbuf(ctx, "place", [P, 2, RING * TPC, 2])
            apart = sbuf(ctx, "apart", [P, 2, RING * TPC, 2, KS])
            hat = sbuf(ctx, "hat", [P, 2, RING * TPC, 2, KS])
            one = sbuf(ctx, "one", [P, 1])
            w_lo = sbuf(ctx, "w_lo", [P, KS, D])
            w_hi = sbuf(ctx, "w_hi", [D, KS, D])
            onT = sbuf(ctx, "onT_2", [P, 2, CE])
            same = sbuf(ctx, "same_2", [P, 2, TPC, P])
            U = sbuf(ctx, "U", [P, 2, TPC, KS, D])
            U_lo = sbuf(ctx, "U_lo", [P, 2, CE])
            U_hi = sbuf(ctx, "U_hi", [D, 2, CE])
            V = sbuf(ctx, "V", [P, TPC, KS, D])
            msg = sbuf(ctx, "msg", [P, 2, TPC, D])
            back = sbuf(ctx, "back_2", [P, RING, TPC, D])
            ps_g = [psum(ctx, f"ps_g2{k}", 512) for k in range(2)]
            ps_lo = psum(ctx, "ps_lo", 512)
            ps_hi = psum(ctx, "ps_hi", 512)
            ps_v = [psum(ctx, f"ps_v{k}", 512) for k in range(2)]
            ps_d = [psum(ctx, f"ps_d2{k}", 512) for k in range(2)]
            idx_in, edges_in, uniq_in = (sems(ctx, n) for n in ("p_idx", "p_edges", "p_uniq"))
            scattered = sems(ctx, "p_scattered", TPC)
            names = ("p_w", "p_pseudo", "p_place", "p_apart", "p_abs", "p_hat", "p_onT", "p_same", "p_got", "p_U",
                     "p_turned", "p_UT", "p_V", "p_VB", "p_msg", "p_dsum", "p_back", "p_xr", "p_xd", "p_tick",
                     "p_done", "p_knots")
            w_in, pseudo_in, place_ok, apart_ok, abs_ok, hat_ok, onT_ok, same_ok, got, U_ok, turned, UT_ok, V_ok, \
                VB_ok, msg_ok, dsummed, back_ok, x_ready, x_done, tick, done, knots_ok = (sem(ctx, n) for n in names)
            w_rows = t["L2_gnn_weight"].rearrange("(k1 k0) i o -> k0 i k1 o", k0=KS)
            with nc.Block() as block:
                @block.sync
                def _(sp):
                    for k0 in range(KS - 1):
                        sp.dma_start(w_lo[k0 * D:(k0 + 1) * D, :, :], w_rows[k0]).then_inc(w_in, 16)
                    sp.dma_start(w_hi[:], w_rows[KS - 1]).then_inc(w_in, 16)

                    def load(i, r, reused):
                        c = i * RING + r
                        if reused:
                            sp.wait_ge(done, c - RING + 1)
                            went_on(sp, sp_went_on)
                        if r == 0:
                            sp.dma_start(pseudo[:, 0, :, :].rearrange("p (c j) f -> p c (j f)", c=RING),
                                         pseudo_chunks[bass.ds(i * RING, RING)].rearrange("c p f -> p c f")
                                         ).then_inc(pseudo_in, 16)
                        sp.dma_start(idx[:, r, :], src_chunks[c]).then_inc(idx_in[r], 16)
                        sp.dma_start(dst_row[:, r, :], dst_rows[c].to_broadcast([P, CE])).then_inc(edges_in[r], 16)
                        sp.dma_start(src_row[:, r, :], src_rows[c].to_broadcast([P, CE])).then_inc(edges_in[r], 16)
                        if reused:
                            for j in range(TPC):
                                sp.wait_ge(scattered[j], (c - RING + 1) * 16)
                                went_on(sp, sp_went_on)
                        sp.dma_start(uniq_idx[:, r, :], cols(uniq, c, TPC)).then_inc(uniq_in[r], 16)

                    for r in range(RING):
                        load(0, r, False)
                    with sp.Fori(1, IT) as i:
                        for r in range(RING):
                            load(i, r, True)
                    for j in range(TPC):
                        sp.wait_ge(scattered[j], 16 * CH)

                @block.gpsimd
                def _(pool):
                    pool.iota(knots[:], [[1, KS]], base=0, channel_multiplier=0,
                              allow_small_or_imprecise_dtypes=True).then_inc(knots_ok, 1)

                    def put(i, r):
                        scatter(pool, i * RING + r, i, r, back_ok, uniq_in, scattered, spline_sums, uniq_idx,
                                lambda r, j: back[:, r, j, :], tick)

                    for r in range(RING):
                        put(0, r)
                    with pool.Fori(1, IT) as i:
                        for r in range(RING):
                            put(i, r)

                @block.scalar
                def _(act):
                    act.wait_ge(knots_ok, 2)
                    with act.Fori(0, IT) as i:
                        act.wait_ge(apart_ok, i + 1)
                        flat_a = apart[:, 0].rearrange("p e d k -> p (e d k)")
                        flat_h = hat[:, 0].rearrange("p e d k -> p (e d k)")
                        act.activation(flat_a, flat_a, ACT.Abs).then_inc(abs_ok, 1)
                        act.wait_ge(abs_ok, i + 1)
                        act.activation(flat_h, flat_a, ACT.Relu, bias=one[:], scale=-1.0).then_inc(hat_ok, 1)
                        for r in range(RING):
                            c = i * RING + r
                            act.wait_ge(turned, c + 1)
                            act.copy(U_lo[:, r % 2, :], ps_lo[:])
                            act.copy(U_hi[:, r % 2, :], ps_hi[0:D, :]).then_inc(UT_ok, 1)
                            act.wait_ge(dsummed, c + 1)
                            act.wait_ge(uniq_in[r], i * 16 + 16)
                            act.copy(back[:, r, :, :], ps_d[r % 2][:, 0:TPC * D].rearrange("p (j f) -> p j f", j=TPC)
                                     ).then_inc(back_ok, 1)

                @block.tensor
                def _(pe):
                    regs = [pe.alloc_register("p_first"), pe.alloc_register("p_last")]
                    n_extra = pe.alloc_register("p_extras")
                    pe.reg_mov(n_extra, 0)
                    pe.wait_ge(w_in, 16 * KS)

                    def read(r, b, start):
                        for j in range(TPC):
                            last = pe.matmul(ps_g[r % 2][:, j * D:(j + 1) * D], onT[:, r % 2, j * P:(j + 1) * P],
                                             X[:, bass.ds(b, 1), :].rearrange("p o f -> p (o f)"),
                                             start=start and j == 0, stop=True, skip_group_check=True)
                        return last

                    with pe.Fori(0, IT) as i:
                        for r in range(RING):
                            c = i * RING + r
                            first, last = block_range(pe, regs, c)
                            pe.wait_ge(onT_ok, c + 1)
                            read(r, first, True).then_inc(got, 1)
                            with pe.If_lt(regs[0], regs[1]):
                                with pe.Fori(first + 1, last + 1) as b:
                                    pe.reg_add(n_extra, n_extra, 1)
                                    k = pe.snap(n_extra)
                                    pe.wait_ge(x_ready, k)
                                    read(r, b, False).then_inc(x_done, 1)
                            pe.wait_ge(U_ok, c + 1)
                            for j in range(TPC):
                                u = U[:, r % 2, j, :, :].rearrange("p k f -> p (k f)")
                                pe.transpose(ps_lo[:, j * P:(j + 1) * P], u[:, 0:P], ident[:])
                                last_mm = pe.transpose(ps_hi[0:D, j * P:(j + 1) * P], u[:, P:], ident[:])
                            last_mm.then_inc(turned, 1)
                            pe.wait_ge(UT_ok, c + 1)
                            for j in range(TPC):
                                o = ps_v[j // 2][:, (j % 2) * KS * D:(j % 2 + 1) * KS * D]
                                pe.matmul(o, U_lo[:, r % 2, j * P:(j + 1) * P], w_lo[:].rearrange("k a o -> k (a o)"),
                                          start=True, stop=False)
                                last_mm = pe.matmul(o, U_hi[:, r % 2, j * P:(j + 1) * P],
                                                    w_hi[:].rearrange("k a o -> k (a o)"), start=False, stop=True)
                            last_mm.then_inc(V_ok, 1)
                            pe.wait_ge(same_ok, c + 1)
                            pe.wait_ge(msg_ok, c + 1)
                            for j in range(TPC):
                                last_mm = pe.matmul(ps_d[r % 2][:, j * D:(j + 1) * D], same[:, r % 2, j, :],
                                                    msg[:, r % 2, j, :], start=True, stop=True)
                            last_mm.then_inc(dsummed, 1)

                @block.vector
                def _(dve):
                    dve.memset(one[:], 1.0).then_inc(knots_ok, 1)
                    dve.wait_ge(knots_ok, 2)
                    regs = [dve.alloc_register("pv_first"), dve.alloc_register("pv_last")]
                    n_extra = dve.alloc_register("pv_extras")
                    dve.reg_mov(n_extra, 0)
                    with dve.Fori(0, IT) as i:
                        dve.wait_ge(pseudo_in, i * 16 + 16)
                        dve.tensor_scalar(place[:, 0], pseudo[:, 0], float(KS - 1), 0.0, ALU.mult,
                                          ALU.max).then_inc(place_ok, 1)
                        dve.wait_ge(place_ok, i * 2 + 1)
                        dve.tensor_scalar(place[:, 0], place[:, 0], float(KS - 1), None, ALU.min).then_inc(place_ok, 1)
                        dve.wait_ge(place_ok, i * 2 + 2)
                        dve.tensor_tensor(apart[:, 0].rearrange("p e d k -> p (e d) k"),
                                          place[:, 0].rearrange("p e d -> p (e d)").unsqueeze(2)
                                          .to_broadcast([P, RING * TPC * 2, KS]),
                                          knots[:].unsqueeze(1).to_broadcast([P, RING * TPC * 2, KS]),
                                          ALU.subtract).then_inc(apart_ok, 1)
                        for r in range(RING):
                            c = i * RING + r
                            h = hat[:, 0, r * TPC:(r + 1) * TPC]
                            first, last = block_range(dve, regs, c)
                            dve.wait_ge(edges_in[r], i * 32 + 32)
                            one_hot_T(onT[:, r % 2, :], dst_row[:, r, :], first).then_inc(onT_ok, 1)
                            dve.wait_ge(idx_in[r], i * 16 + 16)
                            same_src(same[:, r % 2, :, :], src_row[:, r, :], idx[:, r, :]).then_inc(same_ok, 1)
                            dve.wait_ge(got, c + 1)
                            went_on(dve, dve_went_on)
                            with dve.If_lt(regs[0], regs[1]):
                                with dve.Fori(first + 1, last + 1) as b:
                                    dve.reg_add(n_extra, n_extra, 1)
                                    k = dve.snap(n_extra)
                                    one_hot_T(onT[:, r % 2, :], dst_row[:, r, :], b).then_inc(x_ready, 1)
                                    dve.wait_ge(x_done, k)
                            if r == 0:
                                dve.wait_ge(hat_ok, i + 1)
                            for j in range(TPC):
                                last_u = dve.tensor_tensor(
                                    U[:, r % 2, j], h[:, j, 0, :].unsqueeze(2).to_broadcast([P, KS, D]),
                                    ps_g[r % 2][:, j * D:(j + 1) * D].unsqueeze(1).to_broadcast([P, KS, D]), ALU.mult)
                            last_u.then_inc(U_ok, 1)
                            dve.wait_ge(V_ok, c + 1)
                            for q in range(2):
                                last_v = dve.tensor_tensor(
                                    V[:, 2 * q:2 * q + 2],
                                    ps_v[q][:, 0:2 * KS * D].rearrange("p (j k o) -> p j k o", j=2, k=KS),
                                    h[:, 2 * q:2 * q + 2, 1, :].unsqueeze(3).to_broadcast([P, 2, KS, D]), ALU.mult)
                            last_v.then_inc(VB_ok, 1)
                            dve.wait_ge(VB_ok, c + 1)
                            dve.tensor_reduce(msg[:, r % 2], V[:].rearrange("p j k o -> p j o k"), AX,
                                              ALU.add).then_inc(msg_ok, 1)
                            dve.wait_ge(dsummed, c + 1)
                            dve.sem_inc(done, 1)

        with ExitStack() as ctx:
            tmp = sbuf(ctx, "tmp2", [P, NB, D])
            small = sbuf(ctx, "small2", [P, 2, NB])
            part = sbuf(ctx, "part2", [P, 2, NB, D])
            total = sbuf(ctx, "total2", [P, NB, D])
            w_root = sbuf(ctx, "w_root", [D + 1, D])
            xs = sbuf(ctx, "xs2", [P, GB, D])
            xT = sbuf(ctx, "xT2", [D + 1, GB * P])
            ps_t = psum(ctx, "ps_t3", 1024)
            ps_m = psum(ctx, "ps_m3", 512)
            names = ("n2_step", "n2_rf", "n2_ro", "n2_w", "n2_sum", "n2_xs", "n2_t", "n2_xT", "n2_m", "n2_x", "n2_one",
                     "n2_out")
            step, root_from, root_ok, w_in, part_sum, xs_ok, t_ok, xT_ok, m_ok, x_ok, one_ok, table_ok = \
                (sem(ctx, n) for n in names)
            normed = sem(ctx, "n2_normed")
            part_in = sems(ctx, "n2_part", 2)
            with nc.Block() as block:
                @block.sync
                def _(sp):
                    sp.dma_start(w_root[0:D, :], t["L2_gnn_root_weight"]).then_inc(w_in, 16)
                    sp.dma_start(w_root[D:, :], t["L2_gnn_bias"].unsqueeze(0)).then_inc(w_in, 16)
                    for j in range(TPC):
                        if j >= 2:
                            sp.wait_ge(part_sum, j - 1)
                        sp.dma_start(part[:, j % 2, :, :], spline_sums[j][0:NP, :].rearrange("(b p) f -> p b f", p=P)
                                     ).then_inc(part_in[j % 2], 16)
                    sp.wait_ge(normed, 1)
                    sp.dma_start(x3_rows.rearrange("(b p) f -> p b f", p=P), X[:]).then_inc(table_ok, 16)
                    sp.wait_ge(table_ok, 16)

                @block.scalar
                def _(act):
                    layernorm_act(act, small, root_ok, root_from)

                @block.tensor
                def _(pe):
                    pe.wait_ge(w_in, 32)
                    pe.wait_ge(one_ok, 1)
                    with pe.Fori(0, NS) as k:
                        pe.wait_ge(xs_ok, k + 1)
                        turn(pe, ps_t, xs, D).then_inc(t_ok, 1)
                        pe.wait_ge(xT_ok, k + 1)
                        for q in range(GB):
                            last = pe.matmul(ps_m[:, q * D:(q + 1) * D], xT[:, q * P:(q + 1) * P], w_root[:],
                                             start=True, stop=True)
                        last.then_inc(m_ok, 1)

                @block.vector
                def _(dve):
                    dve.memset(xT[D:D + 1, :], 1.0).then_inc(one_ok, 1)
                    for j in range(TPC):
                        dve.wait_ge(part_in[j % 2], 16 * (j // 2 + 1))
                        if j:
                            dve.wait_ge(part_sum, j)
                            dve.tensor_tensor(total[:], total[:], part[:, j % 2, :, :], ALU.add).then_inc(part_sum, 1)
                        else:
                            dve.tensor_copy(total[:], part[:, 0, :, :]).then_inc(part_sum, 1)
                    dve.tensor_scalar(small[:, 0, :], deg_src[:], 1.0, None, ALU.max).then_inc(step, 1)
                    dve.wait_ge(step, 1)
                    dve.reciprocal(small[:, 1, :], small[:, 0, :]).then_inc(step, 1)
                    dve.wait_ge(step, 2)
                    dve.wait_ge(part_sum, TPC)
                    dve.tensor_tensor(tmp[:], total[:], small[:, 1, :].unsqueeze(2).to_broadcast([P, NB, D]),
                                      ALU.mult).then_inc(step, 1)
                    with dve.Fori(0, NS) as k:
                        xb = X[:, bass.ds(k * GB, GB), :]
                        dve.tensor_copy(xs[:], xb).then_inc(xs_ok, 1)
                        dve.wait_ge(t_ok, k + 1)
                        dve.tensor_copy(xT[0:D, :], ps_t[0:D, 0:GB * P]).then_inc(xT_ok, 1)
                        dve.wait_ge(m_ok, k + 1)
                        dve.tensor_tensor(xb, xb, ps_m[:, 0:GB * D].rearrange("p (q f) -> p q f", f=D),
                                          ALU.add).then_inc(x_ok, 1)
                    dve.wait_ge(x_ok, NS)
                    dve.wait_ge(step, 3)
                    dve.tensor_tensor(X[:], X[:], tmp[:], ALU.add).then_inc(step, 1)
                    dve.wait_ge(step, 4)
                    layernorm_dve(dve, tmp[:], small, step, 4, root_ok, root_from)
                    dve.sem_inc(normed, 1)

        clear_semaphores()

        with ExitStack() as ctx:
            idx = sbuf(ctx, "idx_3", [P, RING, TPC], I32)
            rows = sbuf(ctx, "rows_3", [P, RING, TPC, D])
            on = sbuf(ctx, "on_3", [P, 2, TPC, P])
            ps_s = [psum(ctx, f"ps_s3{k}", 512) for k in range(2)]
            ps_x = psum(ctx, "ps_x3", 512)
            idx_in, rows_in = (sems(ctx, n) for n in ("g_idx", "g_rows"))
            names = ("g_on", "g_sum", "g_added", "g_xr", "g_xd", "g_xa", "g_tick", "g_done")
            on_ok, summed, added, x_ready, x_done, x_added, tick, done = (sem(ctx, n) for n in names)
            with nc.Block() as block:
                @block.sync
                def _(sp):
                    with sp.Fori(0, IT) as i:
                        for r in range(RING):
                            c = i * RING + r
                            sp.wait_ge(done, c + 1)
                            went_on(sp, sp_went_on)
                            sp.dma_start(idx[:, r, :], src_chunks[c]).then_inc(idx_in[r], 16)

                @block.gpsimd
                def _(pool):
                    with pool.Fori(0, IT) as i:
                        for r in range(RING):
                            gather(pool, i, r, idx_in, lambda r, j: rows[:, r, j, :], x3_rows, idx, rows_in, tick)

                @block.tensor
                def _(pe):
                    regs = [pe.alloc_register("g_first"), pe.alloc_register("g_last")]
                    n_extra = pe.alloc_register("g_extras")
                    pe.reg_mov(n_extra, 0)

                    def add_up(out, r):
                        for j in range(TPC):
                            last = pe.matmul(out[:, 0:D], on[:, r % 2, j, :], rows[:, r, j, :],
                                             start=j == 0, stop=j == TPC - 1)
                        return last

                    with pe.Fori(0, IT) as i:
                        for r in range(RING):
                            c = i * RING + r
                            first, last = block_range(pe, regs, c)
                            pe.wait_ge(on_ok, c + 1)
                            pe.wait_ge(rows_in[r], i * (16 * TPC) + 16 * TPC)
                            add_up(ps_s[r % 2], r).then_inc(summed, 1)
                            with pe.If_lt(regs[0], regs[1]):
                                with pe.Fori(first + 1, last + 1) as b:
                                    pe.reg_add(n_extra, n_extra, 1)
                                    k = pe.snap(n_extra)
                                    pe.wait_ge(x_ready, k)
                                    add_up(ps_x, r).then_inc(x_done, 1)

                @block.vector
                def _(dve):
                    regs = [dve.alloc_register("gv_first"), dve.alloc_register("gv_last")]
                    n_extra = dve.alloc_register("gv_extras")
                    dve.reg_mov(n_extra, 0)
                    dve.sem_inc(done, RING)
                    with dve.Fori(0, IT) as i:
                        for r in range(RING):
                            c = i * RING + r
                            first, last = block_range(dve, regs, c)
                            one_hot(on[:, r % 2, :, :], c, first).then_inc(on_ok, 1)
                            dve.wait_ge(summed, c + 1)
                            add_to_block(first, D, ps_s[r % 2][:, 0:D]).then_inc(added, 1)
                            went_on(dve, dve_went_on)
                            with dve.If_lt(regs[0], regs[1]):
                                with dve.Fori(first + 1, last + 1) as b:
                                    dve.reg_add(n_extra, n_extra, 1)
                                    k = dve.snap(n_extra)
                                    one_hot(on[:, r % 2, :, :], c, b).then_inc(x_ready, 1)
                                    dve.wait_ge(x_done, k)
                                    add_to_block(b, D, ps_x[:, 0:D]).then_inc(x_added, 1)
                                    dve.wait_ge(x_added, k)
                            dve.wait_ge(added, c + 1)
                            dve.sem_inc(done, 1)

        with ExitStack() as ctx:
            tmp = sbuf(ctx, "tmp3", [P, NB, D])
            small = sbuf(ctx, "small3", [P, 2, NB])
            w = sbuf(ctx, "w3", [2 * D + 1, D])
            xs = sbuf(ctx, "xs3", [P, GB, 2 * D])
            xT = sbuf(ctx, "xT3", [2 * D + 1, GB * P])
            h = sbuf(ctx, "h3", [P, GB, D])
            ps_t = psum(ctx, "ps_t4", 1024)
            ps_m = psum(ctx, "ps_m4", 512)
            names = ("n3_step", "n3_rf", "n3_ro", "n3_w", "n3_xs", "n3_t", "n3_xT", "n3_m", "n3_h", "n3_x", "n3_one",
                     "n3_norm", "n3_out")
            step, root_from, root_ok, w_in, xs_ok, t_ok, xT_ok, m_ok, h_ok, x_ok, one_ok, normed, out_ok = \
                (sem(ctx, n) for n in names)
            with nc.Block() as block:
                @block.sync
                def _(sp):
                    sp.dma_start(w[0:2 * D, :], t["L3_gnn_W"]).then_inc(w_in, 16)
                    sp.dma_start(w[2 * D:, :], t["L3_gnn_b"].unsqueeze(0)).then_inc(w_in, 16)
                    sp.wait_ge(normed, 1)
                    sp.dma_start(t["out"].rearrange("(b p) f -> p b f", p=P), X[:]).then_inc(out_ok, 16)
                    sp.wait_ge(out_ok, 16)

                @block.scalar
                def _(act):
                    with act.Fori(0, NS) as k:
                        act.wait_ge(m_ok, k + 1)
                        act.activation(h[:], ps_m[:, 0:GB * D].rearrange("p (q f) -> p q f", f=D),
                                       ACT.Relu).then_inc(h_ok, 1)
                    layernorm_act(act, small, root_ok, root_from)

                @block.tensor
                def _(pe):
                    pe.wait_ge(w_in, 32)
                    pe.wait_ge(one_ok, 1)
                    with pe.Fori(0, NS) as k:
                        pe.wait_ge(xs_ok, k + 1)
                        went_on(pe, pe_went_on)
                        turn(pe, ps_t, xs, 2 * D).then_inc(t_ok, 1)
                        pe.wait_ge(xT_ok, k + 1)
                        for q in range(GB):
                            last = pe.matmul(ps_m[:, q * D:(q + 1) * D], xT[:, q * P:(q + 1) * P], w[:],
                                             start=True, stop=True)
                        last.then_inc(m_ok, 1)

                @block.vector
                def _(dve):
                    dve.memset(xT[2 * D:2 * D + 1, :], 1.0).then_inc(one_ok, 1)
                    dve.tensor_scalar(small[:, 0, :], deg_dst[:], 1.0, None, ALU.max).then_inc(step, 1)
                    dve.wait_ge(step, 1)
                    dve.reciprocal(small[:, 1, :], small[:, 0, :]).then_inc(step, 1)
                    dve.wait_ge(step, 2)
                    dve.tensor_tensor(tmp[:], acc[:, :, 0:D], small[:, 1, :].unsqueeze(2).to_broadcast([P, NB, D]),
                                      ALU.mult).then_inc(step, 1)
                    dve.wait_ge(step, 3)
                    with dve.Fori(0, NS) as k:
                        xb = X[:, bass.ds(k * GB, GB), :]
                        dve.tensor_copy(xs[:, :, 0:D], xb)
                        dve.tensor_copy(xs[:, :, D:], tmp[:, bass.ds(k * GB, GB), :]).then_inc(xs_ok, 1)
                        dve.wait_ge(t_ok, k + 1)
                        dve.tensor_copy(xT[0:2 * D, :], ps_t[0:2 * D, 0:GB * P]).then_inc(xT_ok, 1)
                        dve.wait_ge(h_ok, k + 1)
                        dve.tensor_tensor(xb, xb, h[:], ALU.add).then_inc(x_ok, 1)
                    dve.wait_ge(x_ok, NS)
                    layernorm_dve(dve, tmp[:], small, step, 3, root_ok, root_from)
                    dve.sem_inc(normed, 1)


def gather(pool, i, r, idx_in, slot, table, idx, rows_in, tick):
    pool.wait_ge(idx_in[r], i * 16 + 16)
    pool.sem_inc(tick, 1)
    for j in range(TPC):
        pool.indirect_dma_start(slot(r, j), None, table,
                                bass.IndirectOffsetOnAxis(ap=idx[:, r, j:j + 1], axis=0)).then_inc(rows_in[r], 16)


def scatter(pool, c, i, r, back_ok, uniq_in, scattered, tables_, uniq_idx, slot, tick):
    pool.wait_ge(back_ok, c + 1)
    pool.wait_ge(uniq_in[r], i * 16 + 16)
    for j in range(TPC):
        if not (isinstance(c, int) and c == 0):
            pool.wait_ge(scattered[j], c * 16)
        pool.sem_inc(tick, 1)
        pool.indirect_dma_start(tables_[j], bass.IndirectOffsetOnAxis(ap=uniq_idx[:, r, j:j + 1], axis=0),
                                slot(r, j), None, compute_op=ALU.add).then_inc(scattered[j], 16)


def tables(pool, n, idx_in, row_slot, rows_table, idx, rows_in, back_ok, uniq_in, scattered, sum_tables, uniq_idx,
           back_slot, tick):
    def put(c, i, r):
        scatter(pool, c, i, r, back_ok, uniq_in, scattered, sum_tables, uniq_idx, back_slot, tick)

    for r in range(RING):
        gather(pool, 0, r, idx_in, row_slot, rows_table, idx, rows_in, tick)
        if r >= LAG:
            put(r - LAG, 0, r - LAG)
    with pool.Fori(1, n) as i:
        for r in range(RING):
            gather(pool, i, r, idx_in, row_slot, rows_table, idx, rows_in, tick)
            if r >= LAG:
                put(i * RING + (r - LAG), i, r - LAG)
            else:
                put(i * RING + (r - LAG), i - 1, r - LAG + RING)
    for r in range(RING - LAG, RING):
        put((n - 1) * RING + r, n - 1, r)


WEIGHTS = ["L0_gnn_attn_w", "L1_gnn_Wf1", "L1_gnn_bf1", "L1_gnn_Wf2", "L1_gnn_bf2", "L1_gnn_Wn1", "L1_gnn_bn1",
           "L1_gnn_Wn2", "L1_gnn_bn2", "L2_gnn_weight", "L2_gnn_root_weight", "L2_gnn_bias", "L3_gnn_W", "L3_gnn_b"]


def kernel(**inputs):
    import concourse.bacc as bacc
    from concourse.bass_utils import run_bass_kernel_spmd

    nc = bacc.Bacc("TRN2", target_bir_lowering=False, num_devices=1)
    arrays = {}
    for name, rows, fill in (("x", NP, 0), ("src", EP, NP - 1), ("dst", EP, NP - 1), ("edge_attr_16", EP, 0),
                             ("edge_attr_2", EP, 0)):
        a = np.asarray(inputs[name])
        padded = np.full((rows, *a.shape[1:]), fill, a.dtype)
        padded[:a.shape[0]] = a
        arrays[name] = padded
    for name in WEIGHTS:
        arrays[name] = np.ascontiguousarray(inputs[name])
    t = {n: nc.dram_tensor(f"in_{n}", a.shape, mybir.dt.from_np(a.dtype), kind="ExternalInput").ap()
         for n, a in arrays.items()}
    t["out"] = nc.dram_tensor("out_x", (NP, D), F32, kind="ExternalOutput").ap()
    build(nc, t)
    r = run_bass_kernel_spmd(nc, [{f"in_{n}": a for n, a in arrays.items()}], core_ids=[0])
    return r.results[0]["out_x"][:N]
```

```python
from contextlib import ExitStack

import numpy as np
import concourse.bass as bass
from concourse import mybir

F32 = mybir.dt.float32
I32 = mybir.dt.int32
I16 = mybir.dt.int16
BF16 = mybir.dt.bfloat16
ALU = mybir.AluOpType
ACT = mybir.ActivationFunctionType
AX = mybir.AxisListType.X

P = 128
N = 12500
E = 400000
D = 32
NB = -(-N // P)
NP = NB * P
TPC = 4
CE = P * TPC
RING = 4
PAIR = 2
CH = -(-E // (CE * RING * PAIR)) * RING * PAIR
TB = PAIR * TPC
CB = CH // PAIR
EP = CH * CE
IT = CH // RING
EA = 16
FH = 64
HW = FH + 1
KS = 5
DUMP = NP
TR = NP + P
BIG = 1.0e30
SLOPE = 0.01
EPS = 1e-5
LAG = 2
GB = 7
NS = NB // GB
RG = 112
NG = CH // RG
VW = 256


def build(nc, t):
    with ExitStack() as top:
        of_layer = []

        def sbuf(ctx, name, shape, dt=F32):
            return ctx.enter_context(nc.sbuf_tensor(name, shape, dt))

        def psum(ctx, name, cols):
            return ctx.enter_context(nc.psum_tensor(name, [P, cols], F32))

        def sem(ctx, name):
            handle = nc.alloc_semaphore(name=name)
            if ctx is not top:
                of_layer.append(handle)
            return handle

        def clear_semaphores():
            nc.clear_and_free_semaphores(of_layer)
            nc.all_engine_barrier()
            of_layer.clear()

        def sems(ctx, name, n=RING):
            return [sem(ctx, f"{name}{r}") for r in range(n)]

        pe_went_on, dve_went_on, sp_went_on = (sem(top, n) for n in ("pe_went_on", "dve_went_on", "sp_went_on"))

        def went_on(eng, signal):
            eng.sem_inc(signal, 1)

        ranges_dram = nc.dram_tensor("ranges_dram", (CH, 4), I32, kind="Internal").ap()
        x_gathered = nc.dram_tensor("x_gathered", (CH, P, TPC * D), F32, kind="Internal").ap()
        flow_rows = nc.dram_tensor("flow_rows", (NP, 2 * FH), F32, kind="Internal").ap()
        flow_sums = [nc.dram_tensor(f"flow_sums{j}", (TR, HW), F32, kind="Internal").ap() for j in range(TPC)]
        spline_sums = [nc.dram_tensor(f"spline_sums{j}", (TR, D), F32, kind="Internal").ap() for j in range(TPC)]
        x3_rows = nc.dram_tensor("x3_rows", (NP, D), F32, kind="Internal").ap()

        src_chunks = t["src"].rearrange("(c p j) -> c p j", p=P, j=TPC)
        src_rows = t["src"].rearrange("(c o e) -> c o e", o=1, e=CE)
        dst_rows = t["dst"].rearrange("(c o e) -> c o e", o=1, e=CE)
        dst_pairs = t["dst"].rearrange("(c o e) -> c o e", o=1, e=PAIR * CE)
        attr_chunks = t["edge_attr_16"].rearrange("(c p j) f -> c p (j f)", p=P, j=TPC)
        pseudo_chunks = t["edge_attr_2"].rearrange("(c p j) f -> c p (j f)", p=P, j=TPC)

        X = sbuf(top, "X", [P, NB, D])
        acc = sbuf(top, "acc", [P, NB, HW])
        dst_col = sbuf(top, "dst_col", [P, CH * TPC], I16)
        uniq = sbuf(top, "uniq", [P, CH * TPC], I32)
        node_id = sbuf(top, "node_id", [P, NB])
        iota = sbuf(top, "iota", [P, NP], I16)
        ident = sbuf(top, "ident", [P, P])
        below = sbuf(top, "below", [P, P])
        dump_id = sbuf(top, "dump_id", [P, 1])
        ranges = sbuf(top, "ranges", [1, CH * 4], I32)
        deg_src = sbuf(top, "deg_src", [P, NB])
        deg_dst = sbuf(top, "deg_dst", [P, NB])

        visit_regs = {eng.engine: [[eng.alloc_register(f"first{r}"), eng.alloc_register(f"last{r}")]
                                   for r in range(RING)] for eng in (nc.tensor, nc.vector)}
        visits_seen = {eng.engine: eng.alloc_register("visits_seen") for eng in (nc.tensor, nc.vector)}
        visits_added = nc.vector.alloc_register("visits_added")

        def load_range(eng, c, r, table=ranges):
            eng.load(visit_regs[eng.engine][r], table[0:1, bass.ds(c * 4, 2)])

        def first_block(eng, r):
            return eng.snap(visit_regs[eng.engine][r][0], min_val=0, max_val=NB - 1)

        def further_blocks(eng, r, visit, signal=None, value=None):
            first, last = visit_regs[eng.engine][r]
            with eng.If_lt(first, last):
                if signal is not None:
                    eng.wait_ge(signal, value)
                    went_on(eng, dve_went_on)
                begin = eng.snap(first, min_val=0, max_val=NB - 2)
                end = eng.snap(last, min_val=1, max_val=NB - 1)
                with eng.Fori(begin + 1, end + 1) as b:
                    eng.reg_add(visits_seen[eng.engine], visits_seen[eng.engine], 1)
                    visit(b, eng.snap(visits_seen[eng.engine]))

        def cols(tensor, c, n):
            return tensor[:, bass.ds(c * n, n)]

        def one_hot_T(out, dst_row, b):
            if out.shape[1] == CE:
                out, row = out.rearrange("n (j p) -> n j p", j=TPC), dst_row.rearrange("n (p j) -> n j p", j=TPC)
            else:
                out = out.rearrange("n (g j p) -> n g j p", j=TPC, p=P)
                row = dst_row.rearrange("n (g p j) -> n g j p", j=TPC, p=P)
            return nc.vector.tensor_scalar(out, row,
                                           node_id[:, bass.ds(b, 1)], None, ALU.is_equal)

        def one_hot(out, c, b):
            n = out.shape[1]
            return nc.vector.tensor_tensor(
                out, iota[:, bass.ds(b * P, P)].unsqueeze(1).to_broadcast([P, n, P]),
                cols(dst_col, c, n).unsqueeze(2).to_broadcast([P, n, P]), ALU.is_equal)

        def add_to_block(b, width, sums):
            a = acc[:, bass.ds(b, 1), 0:width].rearrange("p o f -> p (o f)")
            return nc.vector.tensor_tensor(a, a, sums, ALU.add)

        def add_further(r, c, width, on, ps_x, x_ready, x_done, x_added, added, done_from=0):
            def visit(b, k):
                one_hot(on[:, r, :, :], c, b).then_inc(x_ready, 1)
                nc.vector.wait_ge(x_done, k + done_from)
                nc.vector.reg_add(visits_added, visits_added, 1)
                add_to_block(b, width, ps_x[:, 0:width]).then_inc(x_added, 1)
                nc.vector.wait_ge(x_added, nc.vector.snap(visits_added))
            further_blocks(nc.vector, r, visit, added, c + 3)

        def read_further(r, onT, dst_row, x_ready, x_done, got, value):
            def visit(b, k):
                one_hot_T(onT[:, r % 2, :], dst_row[:, r, :], b).then_inc(x_ready, 1)
                nc.vector.wait_ge(x_done, k)
            further_blocks(nc.vector, r, visit, got, value)

        def read_further_apart(r, onT_x, dst_row, x_ready, x_done):
            def visit(b, k):
                nc.vector.wait_ge(x_done, k)
                one_hot_T(onT_x[:], dst_row[:, r, :], b).then_inc(x_ready, 1)
                nc.vector.wait_ge(x_ready, k)
            further_blocks(nc.vector, r, visit)

        def wait_for_visits(dve, x_done):
            dve.wait_ge(x_done, dve.snap(visits_seen[dve.engine]) + 1)

        def same_src(out, src_row, src_col):
            return nc.vector.tensor_tensor(out, src_row.rearrange("q (p j) -> q j p", j=TPC),
                                           src_col.unsqueeze(2).to_broadcast([P, TPC, P]), ALU.is_equal)

        def split(dve, rest, parts, step, v):
            for k in range(3):
                dve.wait_ge(step, v + 2 * k)
                dve.tensor_copy(parts(k), rest).then_inc(step, 1)
                if k < 2:
                    dve.wait_ge(step, v + 2 * k + 1)
                    dve.tensor_tensor(rest, rest, parts(k), ALU.subtract).then_inc(step, 1)

        with ExitStack() as ctx:
            dst_int = sbuf(ctx, "dst_int", [P, CH, TPC], I32)
            low = sbuf(ctx, "low", [P, CH])
            high = sbuf(ctx, "high", [P, CH])
            lh = sbuf(ctx, "lh", [P, NG, 4])
            lh_int = sbuf(ctx, "lh_int", [P, NG, 4], I32)
            ps = [psum(ctx, f"ps_range{k}", 512) for k in range(2)]
            loaded, x_loaded = sem(ctx, "dst_loaded"), sem(ctx, "x_loaded")
            consts, filled = sem(ctx, "consts"), sem(ctx, "filled")
            minmax, turned, reduced = sem(ctx, "minmax"), sem(ctx, "turned"), sem(ctx, "reduced")
            as_int, stored, back = sem(ctx, "as_int"), sem(ctx, "stored"), sem(ctx, "back")
            with nc.Block() as block:
                @block.sync
                def _(sp):
                    dst_cols = t["dst"].rearrange("(c p j) -> p c j", p=P, j=TPC)
                    for g in range(NG):
                        sp.dma_start(dst_int[:, g * RG:(g + 1) * RG, :],
                                     dst_cols[:, g * RG:(g + 1) * RG, :]).then_inc(loaded, 16)
                    sp.dma_start(X[:], t["x"].rearrange("(b p) f -> p b f", p=P)).then_inc(x_loaded, 16)
                    sp.wait_ge(as_int, 2)
                    sp.dma_start(ranges_dram.rearrange("(g q) k -> q g k", g=NG),
                                 lh_int[0:RG, :, :]).then_inc(stored, 16)
                    sp.wait_ge(stored, 16)
                    sp.dma_start(ranges[0:1, :], ranges_dram.rearrange("(o c) k -> o (c k)", o=1)).then_inc(back, 16)
                    sp.wait_ge(back, 16)
                    sp.wait_ge(x_loaded, 16)

                @block.gpsimd
                def _(pool):
                    pool.memset(ident[:], 0.0).then_inc(filled, 1)
                    pool.memset(below[:], 1.0).then_inc(filled, 1)
                    pool.iota(iota[:], [[1, NP]], base=0, channel_multiplier=0,
                              allow_small_or_imprecise_dtypes=True).then_inc(consts, 1)
                    pool.iota(node_id[:], [[P, NB]], base=0, channel_multiplier=1,
                              allow_small_or_imprecise_dtypes=True).then_inc(consts, 1)
                    pool.iota(dump_id[:], [[0, 1]], base=DUMP, channel_multiplier=1,
                              allow_small_or_imprecise_dtypes=True).then_inc(consts, 1)
                    pool.wait_ge(filled, 2)
                    pool.affine_select(out=ident[:], in_=ident[:], compare_op=ALU.not_equal, fill=1.0, base=0,
                                       pattern=[[-1, P]], channel_multiplier=1).then_inc(consts, 1)
                    pool.affine_select(out=below[:], in_=below[:], compare_op=ALU.is_gt, fill=0.0, base=0,
                                       pattern=[[-1, P]], channel_multiplier=1).then_inc(consts, 1)

                @block.vector
                def _(dve):
                    dve.memset(lh[:], 0.0)
                    dve.wait_ge(loaded, 16 * NG)
                    dve.tensor_copy(dst_col[:], dst_int[:].rearrange("p c j -> p (c j)"))
                    dve.tensor_reduce(low[:], dst_int[:], AX, ALU.min).then_inc(minmax, 1)
                    dve.tensor_reduce(high[:], dst_int[:], AX, ALU.max).then_inc(minmax, 1)
                    for g in range(NG):
                        for k, op in enumerate((ALU.min, ALU.max)):
                            dve.wait_ge(turned, 2 * g + k + 1)
                            dve.tensor_reduce(lh[0:RG, g, k:k + 1], ps[k][0:RG, 0:P], AX,
                                              op).then_inc(reduced, 1)
                    dve.wait_ge(reduced, 2 * NG)
                    dve.tensor_copy(lh_int[:], lh[:]).then_inc(as_int, 1)
                    dve.wait_ge(as_int, 1)
                    dve.tensor_single_scalar(lh_int[:], lh_int[:], P.bit_length() - 1,
                                             ALU.arith_shift_right).then_inc(as_int, 1)

                @block.tensor
                def _(pe):
                    pe.wait_ge(consts, 5)
                    pe.wait_ge(minmax, 2)
                    for g in range(NG):
                        for k, v in enumerate((low, high)):
                            if g:
                                pe.wait_ge(reduced, 2 * (g - 1) + k + 1)
                            pe.transpose(ps[k][0:RG, 0:P], v[:, g * RG:(g + 1) * RG],
                                         ident[:]).then_inc(turned, 1)

        with ExitStack() as layer0:
            s_src = sbuf(layer0, "s_src", [P, CH * TPC])
            s_max = sbuf(layer0, "s_max", [P, NB])
            att = sbuf(layer0, "att", [P, NB, 2, 3], BF16)
            w_att = sbuf(layer0, "w_att", [P, 2 * D])
            with ExitStack() as ctx:
                idx = sbuf(ctx, "idx_a", [P, RING, TPC], I32)
                rows = sbuf(ctx, "rows_a", [P, RING, TPC, D])
                dst_row = sbuf(ctx, "dst_row_a", [P, RING, CE], I32)
                xw = sbuf(ctx, "xw", [P, 2, TPC, D])
                s_col = sbuf(ctx, "s_col", [P, RING, TPC])
                mask = sbuf(ctx, "mask", [P, 2, CE])
                masked = sbuf(ctx, "masked", [P, CE])
                top_s = sbuf(ctx, "top_s", [P, 2])
                ps = [psum(ctx, f"ps_s{k}", CE) for k in range(2)]
                w_loaded = sem(ctx, "w_loaded")
                idx_in, rows_in, src_in, kept = (sems(ctx, n) for n in ("a_idx_in", "a_rows_in", "a_src_in", "a_kept"))
                ready, used, weighed, logit = (sem(ctx, n) for n in ("a_ready", "a_used", "a_weighed", "a_logit"))
                spread, masked_ok, max_ok, folded = (sem(ctx, n) for n in ("a_spread", "a_masked", "a_max", "a_folded"))
                extra, tick = sem(ctx, "a_extra"), sem(ctx, "a_tick")
                with nc.Block() as block:
                    @block.sync
                    def _(sp):
                        sp.dma_start(w_att[:], t["L0_gnn_attn_w"].partition_broadcast(P)).then_inc(w_loaded, 16)

                        def load(c, u, r):
                            if reused(c):
                                sp.wait_ge(used, c - RING + 1)
                                went_on(sp, sp_went_on)
                                sp.wait_ge(kept[r], came(u - RING, 1))
                                went_on(sp, sp_went_on)
                            sp.dma_start(idx[:, r, :], src_chunks[c]).then_inc(idx_in[r], 16)
                            sp.dma_start(dst_row[:, r, :], dst_rows[c].to_broadcast([P, CE])).then_inc(src_in[r], 16)

                        staggered(sp, (0, load))
                        for r in range(RING):
                            sp.wait_ge(kept[r], 16 * IT)

                    @block.gpsimd
                    def _(pool):
                        def fetch(c, u, r):
                            gather(pool, u, r, idx_in, lambda r, j: rows[:, r, j, :], t["x"], idx, rows_in, tick)

                        staggered(pool, (0, fetch))

                    @block.scalar
                    def _(act):
                        def keep(c, u, r):
                            act.wait_ge(rows_in[r], came(u, TPC))
                            act.dma_start(x_gathered[c],
                                          rows[:, r, :, :].rearrange("p j f -> p (j f)")).then_inc(kept[r], 16)

                        staggered(act, (0, keep))

                    @block.tensor
                    def _(pe):
                        def spread_out(c, u, r):
                            pe.wait_ge(logit, c + 1)
                            pe.wait_ge(folded, c + 1)
                            for j in range(TPC):
                                last = pe.matmul(ps[r % 2][:, j * P:(j + 1) * P],
                                                 s_col[:, r, j:j + 1].to_broadcast([P, P]), ident[:],
                                                 start=True, stop=True)
                            last.then_inc(spread, 1)

                        staggered(pe, (0, spread_out))

                    @block.vector
                    def _(dve):
                        dve.reg_mov(visits_seen[dve.engine], 0)
                        dve.sem_inc(folded, 2)
                        dve.memset(s_max[:], -BIG).then_inc(ready, 1)
                        dve.wait_ge(ready, 1)
                        dve.wait_ge(w_loaded, 16)

                        def mask_out(r, b):
                            return dve.tensor_scalar(mask[:, r % 2, :].rearrange("n (j p) -> n j p", j=TPC),
                                                     dst_row[:, r, :].rearrange("n (p j) -> n j p", j=TPC),
                                                     node_id[:, bass.ds(b, 1)], -BIG, ALU.not_equal, ALU.mult)

                        def take_max(r):
                            return dve.tensor_tensor_reduce(out=masked[:], in0=ps[r % 2][:], in1=mask[:, r % 2, :],
                                                            scale=1.0, scalar=-BIG, op0=ALU.add, op1=ALU.max,
                                                            accum_out=top_s[:, 0:1])

                        def fold(b):
                            m = s_max[:, bass.ds(b, 1)]
                            return dve.tensor_tensor(m, m, top_s[:, 0:1], ALU.max)

                        def weigh(c, u, r):
                            dve.wait_ge(rows_in[r], came(u, TPC))
                            dve.tensor_tensor(xw[:, r % 2, :, :], rows[:, r, :, :],
                                              w_att[:, 0:D].unsqueeze(1).to_broadcast([P, TPC, D]),
                                              ALU.mult).then_inc(weighed, 1)
                            load_range(dve, c, r)
                            dve.wait_ge(src_in[r], came(u, 1))
                            mask_out(r, first_block(dve, r)).then_inc(masked_ok, 1)
                            dve.wait_ge(weighed, c + 1)
                            dve.tensor_reduce(s_col[:, r, :], xw[:, r % 2, :, :], AX, ALU.add).then_inc(logit, 1)

                        def maxima(c, u, r):
                            dve.wait_ge(logit, c + 1)
                            dve.tensor_copy(cols(s_src, c, TPC), s_col[:, r, :])
                            dve.wait_ge(masked_ok, c + 1)
                            dve.wait_ge(spread, c + 1)
                            went_on(dve, dve_went_on)
                            take_max(r).then_inc(max_ok, 1)
                            dve.wait_ge(max_ok, c + 1)
                            fold(first_block(dve, r)).then_inc(ready, 1)

                            def visit(b, k):
                                dve.wait_ge(ready, c + 2)
                                mask_out(r, b).then_inc(extra, 1)
                                dve.reg_add(visits_added, visits_added, 1)
                                dve.wait_ge(extra, dve.snap(visits_added))
                                went_on(dve, dve_went_on)
                                take_max(r).then_inc(extra, 1)
                                dve.reg_add(visits_added, visits_added, 1)
                                dve.wait_ge(extra, dve.snap(visits_added))
                                fold(b).then_inc(extra, 1)
                                dve.reg_add(visits_added, visits_added, 1)
                                dve.wait_ge(extra, dve.snap(visits_added))

                            further_blocks(dve, r, visit)
                            dve.wait_ge(ready, c + 2)
                            dve.sem_inc(folded, 1)
                            dve.sem_inc(used, 1)

                        dve.reg_mov(visits_added, 0)
                        staggered(dve, (0, weigh), (1, maxima))

            with ExitStack() as ctx:
                xw = sbuf(ctx, "xw_n", [P, NB, D])
                lin = sbuf(ctx, "lin", [P, NB])
                full = sbuf(ctx, "att_full", [P, NB, 2])
                step = sem(ctx, "att_step")
                with nc.Block() as block:
                    @block.vector
                    def _(dve):
                        dve.tensor_tensor(xw[:], X[:], w_att[:, D:2 * D].unsqueeze(1).to_broadcast([P, NB, D]),
                                          ALU.mult).then_inc(step, 1)
                        dve.memset(acc[:], 0.0)
                        dve.wait_ge(step, 1)
                        dve.tensor_reduce(full[:, :, 0], xw[:], AX, ALU.add).then_inc(step, 1)
                        dve.wait_ge(step, 2)
                        dve.tensor_tensor(lin[:], s_max[:], full[:, :, 0], ALU.add).then_inc(step, 1)
                        dve.wait_ge(step, 3)
                        dve.scalar_tensor_tensor(out=full[:, :, 1], in0=lin[:], scalar=SLOPE, in1=lin[:],
                                                 op0=ALU.mult, op1=ALU.max).then_inc(step, 1)
                        split(dve, full[:], lambda k: att[:, :, :, k], step, 4)

            with ExitStack() as ctx:
                rows = sbuf(ctx, "rows_b", [P, RING, TB, D])
                dst_row = sbuf(ctx, "dst_row_b", [P, RING, PAIR * CE], I32)
                pair_ranges = sbuf(ctx, "pair_ranges", [1, CB * 4], I32)
                onT = sbuf(ctx, "onT_b", [P, 2, PAIR * CE], BF16)
                onT_x = sbuf(ctx, "onT_xb", [P, PAIR * CE], BF16)
                node_att = sbuf(ctx, "node_att", [P, 2, TB, 2])
                on = sbuf(ctx, "on_b", [P, RING, TB, P])
                lin = sbuf(ctx, "lin_b", [P, 2, TB])
                logits = sbuf(ctx, "logits", [P, 2, TB])
                shifted = sbuf(ctx, "shifted", [P, 2, TB])
                H = sbuf(ctx, "H_b", [P, RING, TB, D + 1])
                ps_g = [psum(ctx, f"ps_gb{k}", 512) for k in range(2)]
                ps_s = [psum(ctx, f"ps_sb{k}", 512) for k in range(2)]
                ps_x = psum(ctx, "ps_xb", 512)
                rows_in, dst_in = sems(ctx, "b_rows_in"), sems(ctx, "b_dst_in")
                dst_used, pair_ok = sem(ctx, "b_dst_used"), sem(ctx, "b_pair")
                names = ("b_onT", "b_on", "b_got", "b_natt", "b_lin", "b_logit", "b_shift", "b_exp", "b_H",
                         "b_sum", "b_added", "b_xr", "b_xd", "b_xa")
                onT_ok, on_ok, got, node_att_ok, lin_ok, logit_ok, shift_ok, exp_ok, H_ok, summed, added, x_ready, x_done, \
                    x_added = (sem(ctx, n) for n in names)
                with nc.Block() as block:
                    @block.sync
                    def _(sp):
                        def load_dst(c, u, r):
                            sp.wait_ge(dst_used, c + 1)
                            went_on(sp, sp_went_on)
                            sp.dma_start(dst_row[:, r, :],
                                         dst_pairs[c].to_broadcast([P, PAIR * CE])).then_inc(dst_in[r], 16)

                        def load_rows(c, u, r):
                            if reused(c):
                                sp.wait_ge(H_ok, c - RING + 1)
                                went_on(sp, sp_went_on)
                            sp.dma_start(rows[:, r, :, :].rearrange("p (g j) f -> p g (j f)", g=PAIR),
                                         x_gathered[bass.ds(c * PAIR, PAIR)].rearrange("g p f -> p g f")
                                         ).then_inc(rows_in[r], 16)

                        staggered(sp, (0, load_dst), (0, load_rows), chunks=CB)

                    @block.scalar
                    def _(act):
                        def exponentials(c, u, r):
                            act.wait_ge(shift_ok, c + 1)
                            act.activation(H[:, r, :, D], shifted[:, r % 2, :], ACT.Exp).then_inc(exp_ok, 1)

                        staggered(act, (0, exponentials), chunks=CB)

                    @block.tensor
                    def _(pe):
                        pe.reg_mov(visits_seen[pe.engine], 0)
                        pe.wait_ge(pair_ok, 2)
                        pe.sem_inc(x_done, 1)

                        def read(r, onT, b, start):
                            for j in range(TB):
                                last = pe.matmul(ps_g[r % 2][:, 6 * j:6 * j + 6], onT[:, j * P:(j + 1) * P],
                                                 att[:, bass.ds(b, 1), :, :].rearrange("p o k a -> p (o k a)"),
                                                 start=start and j == 0, stop=True, skip_group_check=True)
                            return last

                        def add_up(out, r):
                            for j in range(TB):
                                last = pe.matmul(out[:, 0:D + 1], on[:, r, j, :], H[:, r, j, :],
                                                 start=j == 0, stop=j == TB - 1)
                            return last

                        def read_nodes(c, u, r):
                            load_range(pe, c, r, pair_ranges)
                            pe.wait_ge(onT_ok, c + 1)
                            read(r, onT[:, r % 2, :], first_block(pe, r), True).then_inc(got, 1)

                            def visit(b, k):
                                pe.wait_ge(x_ready, k)
                                read(r, onT_x, b, False).then_inc(x_done, 1)
                            further_blocks(pe, r, visit)

                        def sum_first(c, u, r):
                            pe.wait_ge(added, c + 1)
                            pe.wait_ge(on_ok, c + 1)
                            pe.wait_ge(H_ok, c + 1)
                            add_up(ps_s[r % 2], r).then_inc(summed, 1)

                        def sum_further(c, u, r):
                            def visit(b, k):
                                pe.wait_ge(x_ready, k)
                                add_up(ps_x, r).then_inc(x_done, 1)
                            further_blocks(pe, r, visit)

                        staggered(pe, (0, read_nodes), (2, sum_first), (3, sum_further), chunks=CB)

                    @block.vector
                    def _(dve):
                        dve.reg_mov(visits_seen[dve.engine], 0)
                        dve.reg_mov(visits_added, 0)
                        span = ranges[:].rearrange("o (c g k) -> o c g k", g=PAIR, k=4)
                        joint = pair_ranges[:].rearrange("o (c k) -> o c k", k=4)
                        for k, op in enumerate((ALU.min, ALU.max)):
                            dve.tensor_tensor(joint[:, :, k], span[:, :, 0, k], span[:, :, 1, k],
                                              op).then_inc(pair_ok, 1)
                        dve.wait_ge(pair_ok, 2)
                        dve.sem_inc(dst_used, RING)
                        dve.sem_inc(added, 2)

                        def join_parts(c, u, r):
                            dve.wait_ge(got, c + 1)
                            wait_for_visits(dve, x_done)
                            dve.tensor_reduce(node_att[:, r % 2], ps_g[r % 2][:, 0:6 * TB].rearrange(
                                "p (j k a) -> p j k a", k=2, a=3), AX, ALU.add).then_inc(node_att_ok, 1)

                        def linear(c, u, r):
                            dve.wait_ge(node_att_ok, c + 1)
                            dve.tensor_tensor(lin[:, r % 2, :], node_att[:, r % 2, :, 0], cols(s_src, c, TB),
                                              ALU.add).then_inc(lin_ok, 1)

                        def by_node(c, u, r):
                            load_range(dve, c, r, pair_ranges)
                            dve.wait_ge(dst_in[r], came(u, 1))
                            one_hot_T(onT[:, r % 2, :], dst_row[:, r, :], first_block(dve, r)).then_inc(onT_ok, 1)

                        def leaky(c, u, r):
                            dve.wait_ge(lin_ok, c + 1)
                            dve.scalar_tensor_tensor(out=logits[:, r % 2, :], in0=lin[:, r % 2, :], scalar=SLOPE,
                                                     in1=lin[:, r % 2, :], op0=ALU.mult,
                                                     op1=ALU.max).then_inc(logit_ok, 1)

                        def by_edge(c, u, r):
                            one_hot(on[:, r, :, :], c, first_block(dve, r)).then_inc(on_ok, 1)

                        def shift(c, u, r):
                            dve.wait_ge(logit_ok, c + 1)
                            dve.tensor_tensor(shifted[:, r % 2, :], logits[:, r % 2, :], node_att[:, r % 2, :, 1],
                                              ALU.subtract).then_inc(shift_ok, 1)

                        def weigh(c, u, r):
                            dve.wait_ge(exp_ok, c + 1)
                            dve.wait_ge(rows_in[r], came(u, 1))
                            dve.tensor_tensor(H[:, r, :, 0:D], rows[:, r, :, :],
                                              H[:, r, :, D:D + 1].to_broadcast([P, TB, D]),
                                              ALU.mult).then_inc(H_ok, 1)

                        def further_nodes(c, u, r):
                            read_further_apart(r, onT_x, dst_row, x_ready, x_done)
                            dve.wait_ge(onT_ok, c + 1)
                            dve.sem_inc(dst_used, 1)

                        def add(c, u, r):
                            dve.wait_ge(added, c + 2)
                            dve.wait_ge(summed, c + 1)
                            add_to_block(first_block(dve, r), D + 1, ps_s[r % 2][:, 0:D + 1]).then_inc(added, 1)
                            add_further(r, c, D + 1, on, ps_x, x_ready, x_done, x_added, added, 1)

                        staggered(dve, (1, join_parts), (0, by_node), (1, linear), (2, weigh), (1, leaky), (0, by_edge),
                                  (1, shift), (0, further_nodes), (3, add), chunks=CB)

        def layernorm_dve(dve, tmp, small, step, v, root_ok, root_from):
            mean, var = small[:, 0, :], small[:, 1, :]
            dve.tensor_reduce(mean, X[:], AX, ALU.add).then_inc(step, 1)
            dve.wait_ge(step, v + 1)
            dve.tensor_scalar(mean, mean, 1.0 / D, None, ALU.mult).then_inc(step, 1)
            dve.wait_ge(step, v + 2)
            dve.tensor_tensor(X[:], X[:], mean.unsqueeze(2).to_broadcast([P, NB, D]), ALU.subtract).then_inc(step, 1)
            dve.wait_ge(step, v + 3)
            dve.tensor_tensor(tmp, X[:], X[:], ALU.mult).then_inc(step, 1)
            dve.wait_ge(step, v + 4)
            dve.tensor_reduce(var, tmp, AX, ALU.add).then_inc(step, 1)
            dve.wait_ge(step, v + 5)
            dve.tensor_scalar(var, var, 1.0 / D, EPS, ALU.mult, ALU.add).then_inc(root_from, 1)
            dve.wait_ge(root_ok, 1)
            dve.reciprocal(var, var).then_inc(step, 1)
            dve.wait_ge(step, v + 6)
            dve.tensor_tensor(X[:], X[:], var.unsqueeze(2).to_broadcast([P, NB, D]), ALU.mult).then_inc(step, 1)
            dve.wait_ge(step, v + 7)

        def layernorm_act(act, small, root_ok, root_from):
            act.wait_ge(root_from, 1)
            act.activation(small[:, 1, :], small[:, 1, :], ACT.Sqrt).then_inc(root_ok, 1)

        def turn(pe, out, rows, width):
            for q in range(GB):
                last = pe.transpose(out[0:width, q * P:(q + 1) * P], rows[:, q, :], ident[:])
            return last

        layer1 = top.enter_context(ExitStack())
        flow_dst = sbuf(layer1, "flow_dst", [P, NB, 2 * FH])
        with ExitStack() as ctx:
            tmp = sbuf(ctx, "tmp0", [P, NB, D])
            small = sbuf(ctx, "small0", [P, 2, NB])
            w_ab = sbuf(ctx, "w_ab", [D, 2 * FH])
            zero = sbuf(ctx, "zero", [P, NP // P * HW + HW])
            xs = sbuf(ctx, "xs0", [P, GB, D])
            xT = sbuf(ctx, "xT0", [D, GB * P])
            swapped = sbuf(ctx, "swapped", [P, GB, 2 * FH])
            ps_t = psum(ctx, "ps_t0", 1024)
            ps_m = psum(ctx, "ps_m0", 1024)
            names = ("n0_step", "n0_rf", "n0_ro", "n0_w", "n0_z", "n0_zeroed", "n0_xs", "n0_t", "n0_xT", "n0_m",
                     "n0_d", "n0_sw", "n0_st")
            step, root_from, root_ok, w_in, zero_ok, zeroed, xs_ok, t_ok, xT_ok, m_ok, d_ok, sw_ok, stored = \
                (sem(ctx, n) for n in names)
            with nc.Block() as block:
                @block.sync
                def _(sp):
                    sp.dma_start(w_ab[:, 0:FH], t["L1_gnn_Wf1"][0:D, :]).then_inc(w_in, 16)
                    sp.dma_start(w_ab[:, FH:2 * FH], t["L1_gnn_Wf1"][D:2 * D, :]).then_inc(w_in, 16)
                    sp.wait_ge(zero_ok, 1)
                    for j in range(TPC):
                        sp.dma_start(flow_sums[j].rearrange("(p b) f -> p (b f)", p=P),
                                     zero[:, 0:TR // P * HW]).then_inc(zeroed, 16)
                        sp.dma_start(spline_sums[j].rearrange("(p b) f -> p (b f)", p=P),
                                     zero[:, 0:TR // P * D]).then_inc(zeroed, 16)
                    with sp.Fori(0, NS) as k:
                        sp.wait_ge(sw_ok, k + 1)
                        sp.dma_start(flow_rows[bass.ds(k * (GB * P), GB * P), :].rearrange("(q p) f -> p q f", p=P),
                                     swapped[:]).then_inc(stored, 16)
                    sp.wait_ge(stored, 16 * NS)
                    sp.wait_ge(zeroed, 32 * TPC)

                @block.scalar
                def _(act):
                    layernorm_act(act, small, root_ok, root_from)

                    def swap(k, reused):
                        act.wait_ge(d_ok, k + 1)
                        if reused:
                            act.wait_ge(stored, k * 16)
                        m = flow_dst[:, bass.ds(k * GB, GB), :].rearrange("p q (h f) -> p q h f", h=2)
                        s = swapped[:].rearrange("p q (h f) -> p q h f", h=2)
                        act.copy(s[:, :, 0, :], m[:, :, 1, :])
                        act.copy(s[:, :, 1, :], m[:, :, 0, :]).then_inc(sw_ok, 1)

                    swap(0, False)
                    with act.Fori(1, NS) as k:
                        swap(k, True)

                @block.tensor
                def _(pe):
                    pe.wait_ge(w_in, 32)
                    with pe.Fori(0, NS) as k:
                        pe.wait_ge(xs_ok, k + 1)
                        turn(pe, ps_t, xs, D).then_inc(t_ok, 1)
                        pe.wait_ge(xT_ok, k + 1)
                        for q in range(GB):
                            last = pe.matmul(ps_m[:, q * P:(q + 1) * P], xT[:, q * P:(q + 1) * P], w_ab[:],
                                             start=True, stop=True)
                        last.then_inc(m_ok, 1)

                @block.vector
                def _(dve):
                    dve.memset(zero[:], 0.0).then_inc(zero_ok, 1)
                    dve.tensor_scalar(small[:, 0, :], acc[:, :, D], 1e-30, None, ALU.max).then_inc(step, 1)
                    dve.wait_ge(step, 1)
                    dve.reciprocal(small[:, 1, :], small[:, 0, :]).then_inc(step, 1)
                    dve.wait_ge(step, 2)
                    dve.tensor_tensor(tmp[:], acc[:, :, 0:D], small[:, 1, :].unsqueeze(2).to_broadcast([P, NB, D]),
                                      ALU.mult).then_inc(step, 1)
                    dve.wait_ge(step, 3)
                    dve.tensor_tensor(X[:], X[:], tmp[:], ALU.add).then_inc(step, 1)
                    dve.wait_ge(step, 4)
                    layernorm_dve(dve, tmp[:], small, step, 4, root_ok, root_from)
                    dve.memset(acc[:], 0.0)
                    with dve.Fori(0, NS) as k:
                        dve.tensor_copy(xs[:], X[:, bass.ds(k * GB, GB), :]).then_inc(xs_ok, 1)
                        dve.wait_ge(t_ok, k + 1)
                        dve.tensor_copy(xT[:], ps_t[0:D, 0:GB * P]).then_inc(xT_ok, 1)
                        dve.wait_ge(m_ok, k + 1)
                        dve.tensor_copy(flow_dst[:, bass.ds(k * GB, GB), :],
                                        ps_m[:, 0:GB * 2 * FH].rearrange("p (q f) -> p q f", f=2 * FH)).then_inc(d_ok, 1)

        clear_semaphores()

        with ExitStack() as ctx:
            idx = sbuf(ctx, "idx_1", [P, RING, TPC], I32)
            uniq_idx = sbuf(ctx, "uniq_1", [P, RING, TPC], I32)
            rows = sbuf(ctx, "rows_1", [P, RING, TPC * 2 * FH])
            dst_row = sbuf(ctx, "dst_row_1", [P, RING, CE], I32)
            src_row = sbuf(ctx, "src_row_1", [P, RING, CE], I32)
            attr = sbuf(ctx, "attr", [P, RING, TPC * EA + 1])
            attrT = sbuf(ctx, "attrT", [TPC * EA + 1, 2, P])
            w_c = sbuf(ctx, "w_c", [TPC * EA + 1, TPC, 2, FH])
            onT = sbuf(ctx, "onT_1", [P, 2, CE])
            on = sbuf(ctx, "on_1", [P, RING, TPC, P])
            same = sbuf(ctx, "same_1", [P, RING, TPC, P])
            earlier = sbuf(ctx, "earlier", [P, TPC, P])
            repeats = sbuf(ctx, "repeats", [P, RING, TPC])
            away = sbuf(ctx, "away", [P, RING, TPC])
            H = sbuf(ctx, "H_1", [P, RING, TPC, 2, HW])
            back = sbuf(ctx, "back_1", [P, RING, TPC, HW])
            ps_h = [psum(ctx, f"ps_h{k}", CE) for k in range(2)]
            ps_t = psum(ctx, "ps_t1", 512)
            ps_s = [psum(ctx, f"ps_s1{k}", 512) for k in range(2)]
            ps_d = [psum(ctx, f"ps_d1{k}", 512) for k in range(2)]
            ps_x = psum(ctx, "ps_x1", 512)
            idx_in, rows_in, edges_in = (sems(ctx, n) for n in ("f_idx", "f_rows", "f_edges"))
            before, counted, moved, uniq_ok, drained, away_ok = \
                (sem(ctx, n) for n in ("f_before", "f_counted", "f_moved", "f_uniq", "f_drained", "f_away"))
            scattered = sems(ctx, "f_scattered", TPC)
            names = ("f_w0", "f_w", "f_onT", "f_on", "f_same", "f_got", "f_turned", "f_attrT", "f_pre", "f_H", "f_sum",
                     "f_dsum", "f_back", "f_added", "f_xr", "f_xd", "f_xa", "f_tick", "f_done", "f_ones")
            w_zero, w_in, onT_ok, on_ok, same_ok, got, turned, attrT_ok, pre_ok, H_ok, summed, dsummed, back_ok, \
                added, x_ready, x_done, x_added, tick, done, ones_ok = (sem(ctx, n) for n in names)
            with nc.Block() as block:
                @block.sync
                def _(sp):
                    sp.wait_ge(w_zero, 1)
                    for j in range(TPC):
                        for h in range(2):
                            sp.dma_start(w_c[j * EA:(j + 1) * EA, j, h, :],
                                         t["L1_gnn_Wf1"][2 * D:, :]).then_inc(w_in, 16)
                            sp.dma_start(w_c[TPC * EA:, j, h, :],
                                         t["L1_gnn_bf1"].unsqueeze(0)).then_inc(w_in, 16)
                    sp.wait_ge(ones_ok, 2)

                    def load(c, u, r):
                        if reused(c):
                            sp.wait_ge(done, c - RING + 1)
                            went_on(sp, sp_went_on)
                            sp.wait_ge(pre_ok, c - RING + 1)
                            went_on(sp, sp_went_on)
                        sp.dma_start(idx[:, r, :], src_chunks[c]).then_inc(idx_in[r], 16)
                        sp.dma_start(dst_row[:, r, :], dst_rows[c].to_broadcast([P, CE])).then_inc(edges_in[r], 16)
                        sp.dma_start(attr[:, r, 0:TPC * EA], attr_chunks[c]).then_inc(edges_in[r], 16)
                        sp.dma_start(src_row[:, r, :], src_rows[c].to_broadcast([P, CE])).then_inc(edges_in[r], 16)

                    staggered(sp, (0, load))
                    for j in range(TPC):
                        sp.wait_ge(scattered[j], 16 * CH)

                @block.gpsimd
                def _(pool):
                    pool.sem_inc(drained, RING - 1)

                    def fetch(c, u, r):
                        gather(pool, u, r, idx_in, lambda r, j: rows[:, r, j * 2 * FH:(j + 1) * 2 * FH], flow_rows,
                               idx, rows_in, tick)

                    def put(c, u, r):
                        pool.wait_ge(back_ok, c + 1)
                        pool.wait_ge(uniq_ok, c + 1)
                        scatter(pool, c, r, scattered, flow_sums, uniq_idx, lambda r, j: back[:, r, j, :], tick,
                                drained)

                    staggered(pool, (0, fetch), (LAG, put))

                @block.scalar
                def _(act):
                    def keep_attrT(c, u, r):
                        act.wait_ge(turned, c + 1)
                        act.copy(attrT[:, r % 2, :], ps_t[0:TPC * EA + 1, 0:P]).then_inc(attrT_ok, 1)

                    def give_back(c, u, r):
                        act.wait_ge(dsummed, c + 1)
                        act.wait_ge(drained, c + 1)
                        act.copy(back[:, r, :, :], ps_d[r % 2][:, 0:TPC * HW].rearrange("p (j f) -> p j f", j=TPC)
                                 ).then_inc(back_ok, 1)

                    def hidden(c, u, r):
                        act.wait_ge(pre_ok, c + 1)
                        act.activation(H[:, r, :, :, 0:FH],
                                       ps_h[r % 2][:].rearrange("p (j h f) -> p j h f", j=TPC, h=2),
                                       ACT.Relu).then_inc(H_ok, 1)

                    act.wait_ge(ones_ok, 2)
                    staggered(act, (0, keep_attrT), (1, give_back), (0, hidden))

                @block.tensor
                def _(pe):
                    pe.reg_mov(visits_seen[pe.engine], 0)
                    pe.sem_inc(got, 2)
                    pe.wait_ge(w_in, 16 * 4 * TPC)

                    def read(r, b):
                        for j in range(TPC):
                            last = pe.matmul(ps_h[r % 2][:, j * P:(j + 1) * P], onT[:, r % 2, j * P:(j + 1) * P],
                                             flow_dst[:, bass.ds(b, 1), :].rearrange("p o f -> p (o f)"),
                                             start=False, stop=True, skip_group_check=True)
                        return last

                    def add_up(out, r):
                        for j in range(TPC):
                            last = pe.matmul(out[:, 0:HW], on[:, r, j, :], H[:, r, j, 0, :],
                                             start=j == 0, stop=j == TPC - 1)
                        return last

                    def turn_attr(c, u, r):
                        load_range(pe, c, r)
                        pe.wait_ge(edges_in[r], came(u, 3))
                        pe.transpose(ps_t[0:TPC * EA + 1, 0:P], attr[:, r, :], ident[:]).then_inc(turned, 1)

                    def sum_first(c, u, r):
                        pe.wait_ge(added, c + 1)
                        pe.wait_ge(on_ok, c + 1)
                        pe.wait_ge(same_ok, c + 1)
                        pe.wait_ge(H_ok, c + 1)
                        add_up(ps_s[r % 2], r).then_inc(summed, 1)
                        for j in range(TPC):
                            last = pe.matmul(ps_d[r % 2][:, j * HW:(j + 1) * HW], same[:, r, j, :],
                                             H[:, r, j, 1, :], start=True, stop=True)
                        last.then_inc(dsummed, 1)

                    def before_relu(c, u, r):
                        pe.wait_ge(attrT_ok, c + 1)
                        pe.matmul(ps_h[r % 2][:], attrT[:, r % 2, :], w_c[:].rearrange("k j h f -> k (j h f)"),
                                  start=True, stop=True, skip_group_check=True)
                        pe.wait_ge(onT_ok, c + 1)
                        read(r, first_block(pe, r)).then_inc(got, 1)

                        def visit(b, k):
                            pe.wait_ge(x_ready, k)
                            read(r, b).then_inc(x_done, 1)
                        further_blocks(pe, r, visit)
                        pe.wait_ge(rows_in[r], came(u, TPC))
                        pe.matmul(ps_h[r % 2][:], ident[:], rows[:, r, :],
                                  start=False, stop=True, skip_group_check=True).then_inc(pre_ok, 1)

                    def sum_further(c, u, r):
                        def visit(b, k):
                            pe.wait_ge(x_ready, k)
                            add_up(ps_x, r).then_inc(x_done, 1)
                        further_blocks(pe, r, visit)

                    staggered(pe, (0, turn_attr), (1, sum_first), (0, before_relu), (2, sum_further))

                @block.vector
                def _(dve):
                    dve.memset(w_c[:], 0.0).then_inc(w_zero, 1)
                    dve.memset(attr[:], 1.0).then_inc(ones_ok, 1)
                    dve.memset(H[:], 1.0).then_inc(ones_ok, 1)
                    dve.reg_mov(visits_seen[dve.engine], 0)
                    dve.reg_mov(visits_added, 0)
                    dve.sem_inc(added, 2)

                    def one_hots(c, u, r):
                        load_range(dve, c, r)
                        dve.wait_ge(edges_in[r], came(u, 3))
                        dve.wait_ge(got, c + 1)
                        one_hot_T(onT[:, r % 2, :], dst_row[:, r, :], first_block(dve, r)).then_inc(onT_ok, 1)
                        one_hot(on[:, r, :, :], c, first_block(dve, r)).then_inc(on_ok, 1)
                        dve.wait_ge(idx_in[r], came(u, 1))
                        same_src(same[:, r, :, :], src_row[:, r, :], idx[:, r, :]).then_inc(same_ok, 1)
                        dve.tensor_tensor(away[:, r, :], dump_id[:].to_broadcast([P, TPC]), idx[:, r, :],
                                          ALU.subtract).then_inc(away_ok, 1)
                        dve.wait_ge(same_ok, c + 1)
                        dve.tensor_tensor(earlier[:], same[:, r, :, :],
                                          below[:].unsqueeze(1).to_broadcast([P, TPC, P]),
                                          ALU.mult).then_inc(before, 1)
                        dve.wait_ge(before, c + 1)
                        dve.tensor_reduce(repeats[:, r, :], earlier[:], AX, ALU.add).then_inc(counted, 1)

                    def further_nodes(c, u, r):
                        read_further(r, onT, dst_row, x_ready, x_done, got, c + 3)

                    def unique(c, u, r):
                        dve.wait_ge(away_ok, c + 1)
                        dve.wait_ge(counted, c + 1)
                        dve.scalar_tensor_tensor(out=away[:, r, :], in0=repeats[:, r, :], scalar=1.0,
                                                 in1=away[:, r, :], op0=ALU.min, op1=ALU.mult).then_inc(moved, 1)
                        dve.wait_ge(moved, c + 1)
                        dve.wait_ge(drained, c + 1)
                        dve.tensor_tensor(uniq_idx[:, r, :], away[:, r, :], idx[:, r, :], ALU.add).then_inc(uniq_ok, 1)
                        dve.tensor_tensor(cols(uniq, c, TPC), away[:, r, :], idx[:, r, :], ALU.add).then_inc(done, 1)

                    def add(c, u, r):
                        dve.wait_ge(added, c + 2)
                        dve.wait_ge(summed, c + 1)
                        dve.wait_ge(dsummed, c + 1)
                        add_to_block(first_block(dve, r), HW, ps_s[r % 2][:, 0:HW]).then_inc(added, 1)
                        add_further(r, c, HW, on, ps_x, x_ready, x_done, x_added, added)

                    staggered(dve, (0, one_hots), (0, further_nodes), (0, unique), (2, add))
        layer1.close()

        with ExitStack() as ctx:
            tmp = sbuf(ctx, "tmp1", [P, NB, D])
            small = sbuf(ctx, "small1", [P, 2, NB])
            part = sbuf(ctx, "part1", [P, 2, NB, HW])
            w_f2 = sbuf(ctx, "w_f2", [HW, FH])
            w_n1 = sbuf(ctx, "w_n1", [FH, FH])
            b_n1 = sbuf(ctx, "b_n1", [FH, 1])
            w_n2 = sbuf(ctx, "w_n2", [HW, D])
            hs = sbuf(ctx, "hs", [P, GB, HW])
            hT = sbuf(ctx, "hT", [HW, GB * P])
            fT = sbuf(ctx, "fT", [FH, GB * P])
            zT = sbuf(ctx, "zT", [HW, GB * P])
            ps_t = psum(ctx, "ps_t2", 1024)
            ps_f = psum(ctx, "ps_f2", 1024)
            ps_m = psum(ctx, "ps_m2", 512)
            names = ("n1_step", "n1_rf", "n1_ro", "n1_w", "n1_sum", "n1_hs", "n1_t", "n1_hT", "n1_f", "n1_fT",
                     "n1_z", "n1_zT", "n1_m", "n1_x", "n1_one")
            step, root_from, root_ok, w_in, part_sum, hs_ok, t_ok, hT_ok, f_ok, fT_ok, z_ok, zT_ok, m_ok, x_ok, \
                one_ok = (sem(ctx, n) for n in names)
            part_in = sems(ctx, "n1_part", 2)
            deg_ok = sem(ctx, "n1_deg")
            halves = ((0, 512), (512, GB * P))
            with nc.Block() as block:
                @block.sync
                def _(sp):
                    for dst, src in ((w_f2[0:FH, :], t["L1_gnn_Wf2"]), (w_f2[FH:, :], t["L1_gnn_bf2"].unsqueeze(0)),
                                     (w_n1[:], t["L1_gnn_Wn1"]), (b_n1[:], t["L1_gnn_bn1"].unsqueeze(1)),
                                     (w_n2[0:FH, :], t["L1_gnn_Wn2"]), (w_n2[FH:, :], t["L1_gnn_bn2"].unsqueeze(0))):
                        sp.dma_start(dst, src).then_inc(w_in, 16)
                    for j in range(TPC):
                        if j >= 2:
                            sp.wait_ge(part_sum, 2 * (j - 2) + 2)
                        sp.dma_start(part[:, j % 2, :, :], flow_sums[j][0:NP, :].rearrange("(b p) f -> p b f", p=P)
                                     ).then_inc(part_in[j % 2], 16)

                @block.scalar
                def _(act):
                    act.wait_ge(w_in, 96)
                    with act.Fori(0, NS) as k:
                        act.wait_ge(f_ok, k + 1)
                        act.copy(fT[:], ps_f[0:FH, 0:GB * P]).then_inc(fT_ok, 1)
                        act.wait_ge(z_ok, k + 1)
                        act.activation(zT[0:FH, :], ps_f[0:FH, 0:GB * P], ACT.Relu, bias=b_n1[:]).then_inc(zT_ok, 1)
                    layernorm_act(act, small, root_ok, root_from)

                @block.tensor
                def _(pe):
                    pe.wait_ge(w_in, 96)
                    pe.wait_ge(one_ok, 1)
                    with pe.Fori(0, NS) as k:
                        pe.wait_ge(hs_ok, k + 1)
                        turn(pe, ps_t, hs, HW).then_inc(t_ok, 1)
                        pe.wait_ge(hT_ok, k + 1)
                        for a, z in halves:
                            last = pe.matmul(ps_f[0:FH, a:z], w_f2[:], hT[:, a:z], start=True, stop=True)
                        last.then_inc(f_ok, 1)
                        pe.wait_ge(fT_ok, k + 1)
                        went_on(pe, pe_went_on)
                        for a, z in halves:
                            last = pe.matmul(ps_f[0:FH, a:z], w_n1[:], fT[:, a:z], start=True, stop=True)
                        last.then_inc(z_ok, 1)
                        pe.wait_ge(zT_ok, k + 1)
                        for q in range(GB):
                            last = pe.matmul(ps_m[:, q * D:(q + 1) * D], zT[:, q * P:(q + 1) * P], w_n2[:],
                                             start=True, stop=True)
                        last.then_inc(m_ok, 1)

                @block.vector
                def _(dve):
                    dve.memset(zT[FH:HW, :], 1.0).then_inc(one_ok, 1)
                    dve.tensor_copy(deg_dst[:], acc[:, :, FH]).then_inc(deg_ok, 1)
                    dve.wait_ge(deg_ok, 1)
                    for j in range(TPC):
                        dve.wait_ge(part_in[j % 2], 16 * (j // 2 + 1))
                        if j:
                            dve.wait_ge(part_sum, 2 * j)
                            dve.tensor_tensor(deg_src[:], deg_src[:], part[:, j % 2, :, FH],
                                              ALU.add).then_inc(part_sum, 1)
                        else:
                            dve.tensor_copy(deg_src[:], part[:, 0, :, FH]).then_inc(part_sum, 1)
                        dve.tensor_tensor(acc[:], acc[:], part[:, j % 2, :, :], ALU.add).then_inc(part_sum, 1)
                    dve.wait_ge(part_sum, 2 * TPC)
                    with dve.Fori(0, NS) as k:
                        dve.tensor_copy(hs[:], acc[:, bass.ds(k * GB, GB), :]).then_inc(hs_ok, 1)
                        dve.wait_ge(t_ok, k + 1)
                        dve.tensor_copy(hT[:], ps_t[0:HW, 0:GB * P]).then_inc(hT_ok, 1)
                        dve.wait_ge(m_ok, k + 1)
                        xb = X[:, bass.ds(k * GB, GB), :]
                        dve.tensor_tensor(xb, xb, ps_m[:, 0:GB * D].rearrange("p (q f) -> p q f", f=D),
                                          ALU.add).then_inc(x_ok, 1)
                    dve.wait_ge(x_ok, NS)
                    layernorm_dve(dve, tmp[:], small, step, 0, root_ok, root_from)
                    dve.memset(acc[:], 0.0)

        clear_semaphores()

        with ExitStack() as ctx:
            idx = sbuf(ctx, "idx_2", [P, RING, TPC], I32)
            uniq_idx = sbuf(ctx, "uniq_2", [P, RING, TPC], I32)
            dst_row = sbuf(ctx, "dst_row_2", [P, RING, CE], I32)
            src_row = sbuf(ctx, "src_row_2", [P, RING, CE], I32)
            pseudo = sbuf(ctx, "pseudo", [P, RING, TPC * 2])
            knots = sbuf(ctx, "knots", [P, KS])
            place = sbuf(ctx, "place", [P, RING, TPC * 2])
            apart = sbuf(ctx, "apart", [P, RING, TPC * 2, KS])
            hat = sbuf(ctx, "hat", [P, RING, TPC, 2, KS])
            one = sbuf(ctx, "one", [P, 1])
            w_lo = sbuf(ctx, "w_lo", [P, KS, D])
            w_hi = sbuf(ctx, "w_hi", [P, TPC, KS, D])
            onT = sbuf(ctx, "onT_2", [P, 2, CE], BF16)
            onT_x = sbuf(ctx, "onT_x2", [P, CE], BF16)
            X_parts = sbuf(ctx, "X_parts", [P, NB, 3, D], BF16)
            rest = sbuf(ctx, "rest", [P, NB, D])
            same = sbuf(ctx, "same_2", [P, RING, TPC, P])
            U = sbuf(ctx, "U", [P, 2, TPC, KS - 1, D])
            U_last = sbuf(ctx, "U_last", [P, 2, TPC, D])
            U_lo = sbuf(ctx, "U_lo", [P, 2, CE])
            U_hi = sbuf(ctx, "U_hi", [P, 2, P])
            V = sbuf(ctx, "V", [P, TPC, KS, D])
            msg = sbuf(ctx, "msg", [P, 2, TPC, D])
            back = sbuf(ctx, "back_2", [P, RING, TPC, D])
            ps_g = psum(ctx, "ps_g2", 512)
            ps_lo = psum(ctx, "ps_lo", 512)
            ps_hi = psum(ctx, "ps_hi", 512)
            ps_v = [psum(ctx, f"ps_v{k}", TPC * VW) for k in range(2)]
            ps_d = psum(ctx, "ps_d2", 512)
            drained, w_zero, parted = sem(ctx, "p_drained"), sem(ctx, "p_w0"), sem(ctx, "p_parted")
            idx_in, edges_in = (sems(ctx, n) for n in ("p_idx", "p_edges"))
            scattered = sems(ctx, "p_scattered", TPC)
            names = ("p_w", "p_place", "p_apart", "p_abs", "p_hat", "p_onT", "p_same", "p_got", "p_U",
                     "p_turned", "p_UT", "p_V", "p_VB", "p_msg", "p_dsum", "p_back", "p_xr", "p_xd", "p_tick",
                     "p_done", "p_knots")
            w_in, place_ok, apart_ok, abs_ok, hat_ok, onT_ok, same_ok, got, U_ok, turned, UT_ok, V_ok, \
                VB_ok, msg_ok, dsummed, back_ok, x_ready, x_done, tick, done, knots_ok = (sem(ctx, n) for n in names)
            w_rows = t["L2_gnn_weight"].rearrange("(k1 k0) i o -> k0 i k1 o", k0=KS)
            with nc.Block() as block:
                @block.sync
                def _(sp):
                    for k0 in range(KS - 1):
                        sp.dma_start(w_lo[k0 * D:(k0 + 1) * D, :, :], w_rows[k0]).then_inc(w_in, 16)
                    sp.wait_ge(w_zero, 1)
                    for j in range(TPC):
                        sp.dma_start(w_hi[j * D:(j + 1) * D, j, :, :], w_rows[KS - 1]).then_inc(w_in, 16)

                    def load(c, u, r):
                        if reused(c):
                            sp.wait_ge(done, c - RING + 1)
                            went_on(sp, sp_went_on)
                        sp.dma_start(idx[:, r, :], src_chunks[c]).then_inc(idx_in[r], 16)
                        sp.dma_start(pseudo[:, r, :], pseudo_chunks[c]).then_inc(edges_in[r], 16)
                        sp.dma_start(dst_row[:, r, :], dst_rows[c].to_broadcast([P, CE])).then_inc(edges_in[r], 16)
                        sp.dma_start(src_row[:, r, :], src_rows[c].to_broadcast([P, CE])).then_inc(edges_in[r], 16)

                    staggered(sp, (0, load))
                    for j in range(TPC):
                        sp.wait_ge(scattered[j], 16 * CH)

                @block.gpsimd
                def _(pool):
                    pool.iota(knots[:], [[1, KS]], base=0, channel_multiplier=0,
                              allow_small_or_imprecise_dtypes=True).then_inc(knots_ok, 1)

                    pool.sem_inc(drained, RING - 1)

                    def put(c, u, r):
                        pool.wait_ge(back_ok, c + 2)
                        scatter(pool, c, r, scattered, spline_sums, uniq_idx, lambda r, j: back[:, r, j, :], tick,
                                drained)

                    staggered(pool, (0, put))

                @block.scalar
                def _(act):
                    act.wait_ge(knots_ok, 2)
                    def hats(c, u, r):
                        a = apart[:, r].rearrange("p e k -> p (e k)")
                        act.wait_ge(apart_ok, c + 1)
                        act.activation(a, a, ACT.Abs).then_inc(abs_ok, 1)
                        act.wait_ge(abs_ok, c + 1)
                        act.activation(hat[:, r].rearrange("p j d k -> p (j d k)"), a, ACT.Relu, bias=one[:],
                                       scale=-1.0).then_inc(hat_ok, 1)

                    def keep_UT(c, u, r):
                        act.wait_ge(V_ok, c + 1)
                        act.wait_ge(turned, c + 1)
                        act.copy(U_lo[:, r % 2, :], ps_lo[:])
                        act.copy(U_hi[:, r % 2, :], ps_hi[:, 0:P]).then_inc(UT_ok, 1)

                    def give_back(c, u, r):
                        act.wait_ge(drained, c + 1)
                        act.copy(uniq_idx[:, r, :], cols(uniq, c, TPC))
                        act.wait_ge(dsummed, c + RING + 1)
                        act.copy(back[:, r, :, :], ps_d[:, 0:TPC * D].rearrange("p (j f) -> p j f", j=TPC)
                                 ).then_inc(back_ok, 1)

                    act.sem_inc(back_ok, 1)
                    staggered(act, (0, hats), (1, keep_UT), (3, give_back))

                @block.tensor
                def _(pe):
                    pe.reg_mov(visits_seen[pe.engine], 0)
                    pe.sem_inc(V_ok, 2)
                    pe.sem_inc(dsummed, RING)
                    pe.wait_ge(w_in, 16 * (KS - 1 + TPC))

                    pe.sem_inc(x_done, 1)
                    pe.wait_ge(parted, 6)

                    def read(onT, b, start):
                        for j in range(TPC):
                            for k in range(3):
                                last = pe.matmul(ps_g[:, j * D:(j + 1) * D], onT[:, j * P:(j + 1) * P],
                                                 X_parts[:, bass.ds(b, 1), k, :].rearrange("p o f -> p (o f)"),
                                                 start=start and j == 0 and k == 0, stop=True,
                                                 skip_group_check=True)
                        return last

                    def by_weights(c, u, r):
                        pe.wait_ge(UT_ok, c + 1)
                        pe.wait_ge(msg_ok, c + 1)
                        for j in range(TPC):
                            o = ps_v[r % 2][:, j * VW:j * VW + KS * D]
                            pe.matmul(o, U_lo[:, r % 2, j * P:(j + 1) * P], w_lo[:].rearrange("k a o -> k (a o)"),
                                      start=True, stop=False)
                            last = pe.matmul(o, U_hi[:, r % 2, :], w_hi[:, j, :, :].rearrange("k a o -> k (a o)"),
                                             start=False, stop=True)
                        last.then_inc(V_ok, 1)

                    def turn_U(c, u, r):
                        pe.wait_ge(U_ok, c * 2 + 2)
                        for j in range(TPC):
                            pe.transpose(ps_lo[:, j * P:(j + 1) * P], U[:, r % 2, j, :, :].rearrange("p k f -> p (k f)"),
                                         ident[:])
                        last = pe.transpose(ps_hi[:, 0:P], U_last[:, r % 2, :, :].rearrange("p j f -> p (j f)"), ident[:])
                        last.then_inc(turned, 1)

                    def read_nodes(c, u, r):
                        load_range(pe, c, r)
                        pe.wait_ge(onT_ok, c + 1)
                        read(onT[:, r % 2, :], first_block(pe, r), True).then_inc(got, 1)

                        def visit(b, k):
                            pe.wait_ge(x_ready, k)
                            read(onT_x, b, False).then_inc(x_done, 1)
                        further_blocks(pe, r, visit)

                    def sum_same(c, u, r):
                        pe.wait_ge(msg_ok, c + 3)
                        pe.wait_ge(same_ok, c + 1)
                        pe.wait_ge(back_ok, c + 1)
                        for j in range(TPC):
                            last = pe.matmul(ps_d[:, j * D:(j + 1) * D], same[:, r, j, :], msg[:, r % 2, j, :],
                                             start=True, stop=True)
                        last.then_inc(dsummed, 1)

                    staggered(pe, (2, by_weights), (1, turn_U), (0, read_nodes), (3, sum_same))

                @block.vector
                def _(dve):
                    dve.memset(w_hi[:], 0.0).then_inc(w_zero, 1)
                    dve.tensor_copy(rest[:], X[:]).then_inc(parted, 1)
                    split(dve, rest[:], lambda k: X_parts[:, :, k, :], parted, 1)
                    dve.memset(one[:], 1.0).then_inc(knots_ok, 1)
                    dve.wait_ge(knots_ok, 2)
                    dve.reg_mov(visits_seen[dve.engine], 0)
                    dve.sem_inc(msg_ok, 2)

                    def prepare(c, u, r):
                        load_range(dve, c, r)
                        dve.wait_ge(edges_in[r], came(u, 3))
                        dve.tensor_scalar(place[:, r], pseudo[:, r], float(KS - 1), 0.0, ALU.mult,
                                          ALU.max).then_inc(place_ok, 1)
                        one_hot_T(onT[:, r % 2, :], dst_row[:, r, :], first_block(dve, r)).then_inc(onT_ok, 1)
                        dve.wait_ge(place_ok, c * 2 + 1)
                        dve.tensor_scalar(place[:, r], place[:, r], float(KS - 1), None, ALU.min).then_inc(place_ok, 1)
                        dve.wait_ge(idx_in[r], came(u, 1))
                        dve.wait_ge(dsummed, c + 1)
                        same_src(same[:, r, :, :], src_row[:, r, :], idx[:, r, :]).then_inc(same_ok, 1)
                        dve.wait_ge(place_ok, c * 2 + 2)
                        dve.tensor_tensor(apart[:, r], place[:, r].unsqueeze(2).to_broadcast([P, TPC * 2, KS]),
                                          knots[:].unsqueeze(1).to_broadcast([P, TPC * 2, KS]),
                                          ALU.subtract).then_inc(apart_ok, 1)

                    def spread(c, u, r):
                        dve.wait_ge(hat_ok, c + 1)
                        dve.wait_ge(got, c + 1)
                        wait_for_visits(dve, x_done)
                        x = ps_g[:, 0:TPC * D].rearrange("p (j f) -> p j f", j=TPC)
                        dve.tensor_tensor(U[:, r % 2], hat[:, r, :, 0, 0:KS - 1].unsqueeze(3)
                                          .to_broadcast([P, TPC, KS - 1, D]),
                                          x.unsqueeze(2).to_broadcast([P, TPC, KS - 1, D]), ALU.mult).then_inc(U_ok, 1)
                        dve.tensor_tensor(U_last[:, r % 2], hat[:, r, :, 0, KS - 1:].to_broadcast([P, TPC, D]), x,
                                          ALU.mult).then_inc(U_ok, 1)

                    def message(c, u, r):
                        dve.wait_ge(V_ok, c + 3)
                        dve.wait_ge(msg_ok, c + 2)
                        dve.tensor_tensor(V[:], ps_v[r % 2][:].rearrange("p (j v) -> p j v", j=TPC)[:, :, 0:KS * D]
                                          .rearrange("p j (k o) -> p j k o", k=KS),
                                          hat[:, r, :, 1, :].unsqueeze(3).to_broadcast([P, TPC, KS, D]),
                                          ALU.mult).then_inc(VB_ok, 1)
                        dve.wait_ge(VB_ok, c + 1)
                        dve.wait_ge(dsummed, c + RING - 1)
                        dve.tensor_reduce(msg[:, r % 2], V[:].rearrange("p j k o -> p j o k"), AX,
                                          ALU.add).then_inc(msg_ok, 1)

                    def further_nodes(c, u, r):
                        read_further_apart(r, onT_x, dst_row, x_ready, x_done)
                        dve.wait_ge(apart_ok, c + 1)
                        dve.sem_inc(done, 1)

                    staggered(dve, (0, prepare), (1, spread), (2, message), (0, further_nodes))

        with ExitStack() as ctx:
            tmp = sbuf(ctx, "tmp2", [P, NB, D])
            small = sbuf(ctx, "small2", [P, 2, NB])
            part = sbuf(ctx, "part2", [P, 2, NB, D])
            total = sbuf(ctx, "total2", [P, NB, D])
            w_root = sbuf(ctx, "w_root", [D + 1, D])
            xs = sbuf(ctx, "xs2", [P, GB, D])
            xT = sbuf(ctx, "xT2", [D + 1, GB * P])
            ps_t = psum(ctx, "ps_t3", 1024)
            ps_m = psum(ctx, "ps_m3", 512)
            names = ("n2_step", "n2_rf", "n2_ro", "n2_w", "n2_sum", "n2_xs", "n2_t", "n2_xT", "n2_m", "n2_x", "n2_one",
                     "n2_out")
            step, root_from, root_ok, w_in, part_sum, xs_ok, t_ok, xT_ok, m_ok, x_ok, one_ok, table_ok = \
                (sem(ctx, n) for n in names)
            normed = sem(ctx, "n2_normed")
            part_in = sems(ctx, "n2_part", 2)
            with nc.Block() as block:
                @block.sync
                def _(sp):
                    sp.dma_start(w_root[0:D, :], t["L2_gnn_root_weight"]).then_inc(w_in, 16)
                    sp.dma_start(w_root[D:, :], t["L2_gnn_bias"].unsqueeze(0)).then_inc(w_in, 16)
                    for j in range(TPC):
                        if j >= 2:
                            sp.wait_ge(part_sum, j - 1)
                        sp.dma_start(part[:, j % 2, :, :], spline_sums[j][0:NP, :].rearrange("(b p) f -> p b f", p=P)
                                     ).then_inc(part_in[j % 2], 16)
                    sp.wait_ge(normed, 1)
                    sp.dma_start(x3_rows.rearrange("(b p) f -> p b f", p=P), X[:]).then_inc(table_ok, 16)
                    sp.wait_ge(table_ok, 16)

                @block.scalar
                def _(act):
                    layernorm_act(act, small, root_ok, root_from)

                @block.tensor
                def _(pe):
                    pe.wait_ge(w_in, 32)
                    pe.wait_ge(one_ok, 1)
                    with pe.Fori(0, NS) as k:
                        pe.wait_ge(xs_ok, k + 1)
                        turn(pe, ps_t, xs, D).then_inc(t_ok, 1)
                        pe.wait_ge(xT_ok, k + 1)
                        for q in range(GB):
                            last = pe.matmul(ps_m[:, q * D:(q + 1) * D], xT[:, q * P:(q + 1) * P], w_root[:],
                                             start=True, stop=True)
                        last.then_inc(m_ok, 1)

                @block.vector
                def _(dve):
                    dve.memset(xT[D:D + 1, :], 1.0).then_inc(one_ok, 1)
                    for j in range(TPC):
                        dve.wait_ge(part_in[j % 2], 16 * (j // 2 + 1))
                        if j:
                            dve.wait_ge(part_sum, j)
                            dve.tensor_tensor(total[:], total[:], part[:, j % 2, :, :], ALU.add).then_inc(part_sum, 1)
                        else:
                            dve.tensor_copy(total[:], part[:, 0, :, :]).then_inc(part_sum, 1)
                    dve.tensor_scalar(small[:, 0, :], deg_src[:], 1.0, None, ALU.max).then_inc(step, 1)
                    dve.wait_ge(step, 1)
                    dve.reciprocal(small[:, 1, :], small[:, 0, :]).then_inc(step, 1)
                    dve.wait_ge(step, 2)
                    dve.wait_ge(part_sum, TPC)
                    dve.tensor_tensor(tmp[:], total[:], small[:, 1, :].unsqueeze(2).to_broadcast([P, NB, D]),
                                      ALU.mult).then_inc(step, 1)
                    with dve.Fori(0, NS) as k:
                        xb = X[:, bass.ds(k * GB, GB), :]
                        dve.tensor_copy(xs[:], xb).then_inc(xs_ok, 1)
                        dve.wait_ge(t_ok, k + 1)
                        dve.tensor_copy(xT[0:D, :], ps_t[0:D, 0:GB * P]).then_inc(xT_ok, 1)
                        dve.wait_ge(m_ok, k + 1)
                        dve.tensor_tensor(xb, xb, ps_m[:, 0:GB * D].rearrange("p (q f) -> p q f", f=D),
                                          ALU.add).then_inc(x_ok, 1)
                    dve.wait_ge(x_ok, NS)
                    dve.wait_ge(step, 3)
                    dve.tensor_tensor(X[:], X[:], tmp[:], ALU.add).then_inc(step, 1)
                    dve.wait_ge(step, 4)
                    layernorm_dve(dve, tmp[:], small, step, 4, root_ok, root_from)
                    dve.sem_inc(normed, 1)

        clear_semaphores()

        with ExitStack() as ctx:
            idx = sbuf(ctx, "idx_3", [P, RING, TPC], I32)
            rows = sbuf(ctx, "rows_3", [P, RING, TPC, D])
            on = sbuf(ctx, "on_3", [P, RING, TPC, P])
            ps_s = [psum(ctx, f"ps_s3{k}", 512) for k in range(2)]
            ps_x = psum(ctx, "ps_x3", 512)
            idx_in, rows_in = (sems(ctx, n) for n in ("g_idx", "g_rows"))
            names = ("g_on", "g_sum", "g_added", "g_xr", "g_xd", "g_xa", "g_tick", "g_done")
            on_ok, summed, added, x_ready, x_done, x_added, tick, done = (sem(ctx, n) for n in names)
            with nc.Block() as block:
                @block.sync
                def _(sp):
                    def load(c, u, r):
                        sp.wait_ge(done, c + 1)
                        went_on(sp, sp_went_on)
                        sp.dma_start(idx[:, r, :], src_chunks[c]).then_inc(idx_in[r], 16)

                    staggered(sp, (0, load))

                @block.gpsimd
                def _(pool):
                    def fetch(c, u, r):
                        gather(pool, u, r, idx_in, lambda r, j: rows[:, r, j, :], x3_rows, idx, rows_in, tick)

                    staggered(pool, (0, fetch))

                @block.tensor
                def _(pe):
                    pe.reg_mov(visits_seen[pe.engine], 0)

                    def add_up(out, r):
                        for j in range(TPC):
                            last = pe.matmul(out[:, 0:D], on[:, r, j, :], rows[:, r, j, :],
                                             start=j == 0, stop=j == TPC - 1)
                        return last

                    def sum_first(c, u, r):
                        load_range(pe, c, r)
                        pe.wait_ge(added, c + 1)
                        pe.wait_ge(on_ok, c + 1)
                        pe.wait_ge(rows_in[r], came(u, TPC))
                        add_up(ps_s[r % 2], r).then_inc(summed, 1)

                    def sum_further(c, u, r):
                        def visit(b, k):
                            pe.wait_ge(x_ready, k)
                            add_up(ps_x, r).then_inc(x_done, 1)
                        further_blocks(pe, r, visit)

                    staggered(pe, (0, sum_first), (1, sum_further))

                @block.vector
                def _(dve):
                    dve.reg_mov(visits_seen[dve.engine], 0)
                    dve.reg_mov(visits_added, 0)
                    dve.sem_inc(done, RING)
                    dve.sem_inc(added, 2)

                    def by_edge(c, u, r):
                        load_range(dve, c, r)
                        one_hot(on[:, r, :, :], c, first_block(dve, r)).then_inc(on_ok, 1)

                    def add(c, u, r):
                        dve.wait_ge(added, c + 2)
                        dve.wait_ge(summed, c + 1)
                        add_to_block(first_block(dve, r), D, ps_s[r % 2][:, 0:D]).then_inc(added, 1)
                        add_further(r, c, D, on, ps_x, x_ready, x_done, x_added, added)
                        dve.sem_inc(done, 1)

                    staggered(dve, (0, by_edge), (1, add))

        with ExitStack() as ctx:
            tmp = sbuf(ctx, "tmp3", [P, NB, D])
            small = sbuf(ctx, "small3", [P, 2, NB])
            w = sbuf(ctx, "w3", [2 * D + 1, D])
            xs = sbuf(ctx, "xs3", [P, GB, 2 * D])
            xT = sbuf(ctx, "xT3", [2 * D + 1, GB * P])
            h = sbuf(ctx, "h3", [P, GB, D])
            ps_t = psum(ctx, "ps_t4", 1024)
            ps_m = psum(ctx, "ps_m4", 512)
            names = ("n3_step", "n3_rf", "n3_ro", "n3_w", "n3_xs", "n3_t", "n3_xT", "n3_m", "n3_h", "n3_x", "n3_one",
                     "n3_norm", "n3_out")
            step, root_from, root_ok, w_in, xs_ok, t_ok, xT_ok, m_ok, h_ok, x_ok, one_ok, normed, out_ok = \
                (sem(ctx, n) for n in names)
            with nc.Block() as block:
                @block.sync
                def _(sp):
                    sp.dma_start(w[0:2 * D, :], t["L3_gnn_W"]).then_inc(w_in, 16)
                    sp.dma_start(w[2 * D:, :], t["L3_gnn_b"].unsqueeze(0)).then_inc(w_in, 16)
                    sp.wait_ge(normed, 1)
                    sp.dma_start(t["out"].rearrange("(b p) f -> p b f", p=P), X[:]).then_inc(out_ok, 16)
                    sp.wait_ge(out_ok, 16)

                @block.scalar
                def _(act):
                    with act.Fori(0, NS) as k:
                        act.wait_ge(m_ok, k + 1)
                        act.activation(h[:], ps_m[:, 0:GB * D].rearrange("p (q f) -> p q f", f=D),
                                       ACT.Relu).then_inc(h_ok, 1)
                    layernorm_act(act, small, root_ok, root_from)

                @block.tensor
                def _(pe):
                    pe.wait_ge(w_in, 32)
                    pe.wait_ge(one_ok, 1)
                    with pe.Fori(0, NS) as k:
                        pe.wait_ge(xs_ok, k + 1)
                        went_on(pe, pe_went_on)
                        turn(pe, ps_t, xs, 2 * D).then_inc(t_ok, 1)
                        pe.wait_ge(xT_ok, k + 1)
                        for q in range(GB):
                            last = pe.matmul(ps_m[:, q * D:(q + 1) * D], xT[:, q * P:(q + 1) * P], w[:],
                                             start=True, stop=True)
                        last.then_inc(m_ok, 1)

                @block.vector
                def _(dve):
                    dve.memset(xT[2 * D:2 * D + 1, :], 1.0).then_inc(one_ok, 1)
                    dve.tensor_scalar(small[:, 0, :], deg_dst[:], 1.0, None, ALU.max).then_inc(step, 1)
                    dve.wait_ge(step, 1)
                    dve.reciprocal(small[:, 1, :], small[:, 0, :]).then_inc(step, 1)
                    dve.wait_ge(step, 2)
                    dve.tensor_tensor(tmp[:], acc[:, :, 0:D], small[:, 1, :].unsqueeze(2).to_broadcast([P, NB, D]),
                                      ALU.mult).then_inc(step, 1)
                    dve.wait_ge(step, 3)
                    with dve.Fori(0, NS) as k:
                        xb = X[:, bass.ds(k * GB, GB), :]
                        dve.tensor_copy(xs[:, :, 0:D], xb)
                        dve.tensor_copy(xs[:, :, D:], tmp[:, bass.ds(k * GB, GB), :]).then_inc(xs_ok, 1)
                        dve.wait_ge(t_ok, k + 1)
                        dve.tensor_copy(xT[0:2 * D, :], ps_t[0:2 * D, 0:GB * P]).then_inc(xT_ok, 1)
                        dve.wait_ge(h_ok, k + 1)
                        dve.tensor_tensor(xb, xb, h[:], ALU.add).then_inc(x_ok, 1)
                    dve.wait_ge(x_ok, NS)
                    layernorm_dve(dve, tmp[:], small, step, 3, root_ok, root_from)
                    dve.sem_inc(normed, 1)


def gather(pool, u, r, idx_in, slot, table, idx, rows_in, tick):
    pool.wait_ge(idx_in[r], came(u, 1))
    pool.sem_inc(tick, 1)
    for j in range(TPC):
        pool.indirect_dma_start(slot(r, j), None, table,
                                bass.IndirectOffsetOnAxis(ap=idx[:, r, j:j + 1], axis=0)).then_inc(rows_in[r], 16)


def scatter(pool, c, r, scattered, tables, uniq_idx, slot, tick, drained):
    for j in range(TPC):
        if not (isinstance(c, int) and c == 0):
            pool.wait_ge(scattered[j], c * 16)
        pool.sem_inc(drained if j == TPC - 1 else tick, 1)
        pool.indirect_dma_start(tables[j], bass.IndirectOffsetOnAxis(ap=uniq_idx[:, r, j:j + 1], axis=0),
                                slot(r, j), None, compute_op=ALU.add).then_inc(scattered[j], 16)


def came(u, n):
    return u * (16 * n // RING) + 16 * n


def reused(c):
    return not isinstance(c, int) or c >= RING


def staggered(eng, *stages, chunks=CH):
    for t in range(RING):
        for lag, stage in stages:
            if t >= lag:
                stage(t - lag, 0, t - lag)
    with eng.Fori(RING, chunks - RING + 1, RING) as u:
        for t in range(RING):
            for lag, stage in stages:
                q = t - lag
                stage(u + q, u if q >= 0 else u - RING, q % RING)
    for t in range(max(lag for lag, _ in stages)):
        for lag, stage in stages:
            if lag > t:
                c = chunks + t - lag
                stage(c, c - c % RING, c % RING)


WEIGHTS = ["L0_gnn_attn_w", "L1_gnn_Wf1", "L1_gnn_bf1", "L1_gnn_Wf2", "L1_gnn_bf2", "L1_gnn_Wn1", "L1_gnn_bn1",
           "L1_gnn_Wn2", "L1_gnn_bn2", "L2_gnn_weight", "L2_gnn_root_weight", "L2_gnn_bias", "L3_gnn_W", "L3_gnn_b"]


def kernel(**inputs):
    import concourse.bacc as bacc
    from concourse.bass_utils import run_bass_kernel_spmd

    nc = bacc.Bacc("TRN2", target_bir_lowering=False, num_devices=1)
    arrays = {}
    for name, rows, fill in (("x", NP, 0), ("src", EP, NP - 1), ("dst", EP, NP - 1), ("edge_attr_16", EP, 0),
                             ("edge_attr_2", EP, 0)):
        a = np.asarray(inputs[name])
        padded = np.full((rows, *a.shape[1:]), fill, a.dtype)
        padded[:a.shape[0]] = a
        arrays[name] = padded
    for name in WEIGHTS:
        arrays[name] = np.ascontiguousarray(inputs[name])
    t = {n: nc.dram_tensor(f"in_{n}", a.shape, mybir.dt.from_np(a.dtype), kind="ExternalInput").ap()
         for n, a in arrays.items()}
    t["out"] = nc.dram_tensor("out_x", (NP, D), F32, kind="ExternalOutput").ap()
    build(nc, t)
    r = run_bass_kernel_spmd(nc, [{f"in_{n}": a for n, a in arrays.items()}], core_ids=[0])
    return r.results[0]["out_x"][:N]
```
